# Optimizing a Trainium2 kernel written in Bass

```python
import numpy as np
import jax
import jax.numpy as jnp

def _softmax(x, axis=-1):
    return jax.nn.softmax(x, axis=axis)

def _gelu(x):
    return jax.nn.gelu(x, approximate=True)

def _silu(x):
    return jax.nn.silu(x)

def _sigmoid(x):
    return jax.nn.sigmoid(x)

def _layernorm(x, axis=-1, eps=1e-05):
    m = jnp.mean(x, axis=axis, keepdims=True)
    v = jnp.var(x, axis=axis, keepdims=True)
    return (x - m) / jnp.sqrt(v + eps)

def _scatter_add(tgt, idx, src, axis=0):
    return tgt.at[idx].add(src)

def _segment_sum(src, seg, n):
    return jax.ops.segment_sum(src, seg, n)
kernel_name = 'mk_lm_tower_d2_tok_ids1024_r4_81010e'

def setup_inputs(seed: int=0):
    np.random.seed(seed)
    _w = jnp.asarray

    def _rec_inputs():
        import jax
        import jax.numpy as jnp
        _rk = jax.random.key(seed)
        x = jax.random.randint(jax.random.fold_in(_rk, 1), (64, 128), 0, 64, jnp.int32)
        return x
    x = _rec_inputs()

    def _L0_tok_setup():
        import jax, jax.numpy as jnp
        import numpy as np
        N_FFT = 64
        HOP = 64
        NUM_FREQ = N_FFT // 2 + 1

        def _stft_mag(sig, window):
            L = sig.shape[1]
            pad = N_FFT // 2
            x = jnp.pad(sig, ((0, 0), (pad, pad)), mode='reflect')
            n_frames = 1 + L // HOP
            idx = jnp.arange(n_frames)[:, None] * HOP + jnp.arange(N_FFT)[None, :]
            frames = x[:, idx] * window
            spec = jnp.fft.rfft(frames, axis=-1)
            r, im = (spec.real, spec.imag)
            m2 = r * r + im * im
            mag = jnp.where(m2 == 0, 0.0, jnp.sqrt(jnp.where(m2 == 0, 1.0, m2)))
            return (mag, n_frames)

        def _linear_interp_last(feat, out_len):
            in_len = feat.shape[-1]
            coord = jnp.clip((jnp.arange(out_len) + 0.5) * (in_len / out_len) - 0.5, 0.0, in_len - 1.0)
            i0 = jnp.floor(coord).astype(jnp.int32)
            i1 = jnp.minimum(i0 + 1, in_len - 1)
            w = (coord - i0).astype(feat.dtype)
            return feat[..., i0] * (1.0 - w) + feat[..., i1] * w
        key = jax.random.key(seed)
        k0, k1, k2 = jax.random.split(key, 3)
        B, L, V, d_model = (2, 256, 64, 256)
        d_emb = int(d_model * 0.7)
        d_stft = d_model - d_emb
        input_ids = jax.random.randint(k0, (B, L), 0, V)
        emb_table = jax.random.normal(k1, (V, d_emb), jnp.float32) * 0.02
        proj_w = jax.random.normal(k2, (d_stft, V * NUM_FREQ), jnp.float32) * 0.02
        proj_b = jnp.zeros((d_stft,), jnp.float32)
        n = jnp.arange(N_FFT, dtype=jnp.float32)
        window = 0.5 * (1.0 - jnp.cos(2.0 * jnp.pi * n / N_FFT))
        return {'input_ids': input_ids, 'emb_table': emb_table, 'proj_w': proj_w, 'proj_b': proj_b, 'window': window}
    _L0_tok_all = _L0_tok_setup()
    _L0_tok_in = {k: v for k, v in _L0_tok_all.items() if k in ('emb_table', 'proj_w', 'proj_b', 'window')}
    del _L0_tok_all

    def _L0_attn_setup():
        import jax, jax.numpy as jnp
        import numpy as np
        import math
        D = 256
        H = 16
        HEAD_D = D // H
        T = 512
        B = 4
        key = jax.random.key(seed)
        k1, k2, k3 = jax.random.split(key, 3)
        x = jax.random.normal(k1, (B, T, D), dtype=jnp.float32)
        w_attn = jax.random.normal(k2, (D, D + 2 * HEAD_D), dtype=jnp.float32) * (1.0 / math.sqrt(D))
        w_proj = jax.random.normal(k3, (D, D), dtype=jnp.float32) * (1.0 / math.sqrt(D))
        return {'x': x, 'w_attn': w_attn, 'w_proj': w_proj}
    _L0_attn_all = _L0_attn_setup()
    _L0_attn_in = {k: v for k, v in _L0_attn_all.items() if k in ('w_attn', 'w_proj')}
    del _L0_attn_all

    def _L0_ffn_setup():
        import jax, jax.numpy as jnp
        import numpy as np
        B, S, D_IN, D_OUT = (16, 1024, 256, 256)
        ACT_BITS = 8
        QB = float(2 ** (ACT_BITS - 1) - 1)
        key = jax.random.key(seed)
        k1, k2, k3 = jax.random.split(key, 3)
        x = jax.random.normal(k1, (B, S, D_IN), dtype=jnp.float32)
        ternary_weight = jax.random.randint(k2, (D_OUT, D_IN), 0, 3, dtype=jnp.int32)
        bias = jax.random.normal(k3, (D_OUT,), dtype=jnp.float32)
        act_scale = (jnp.max(jnp.abs(x)) / QB).astype(jnp.float32)
        return {'x': x, 'ternary_weight': ternary_weight, 'bias': bias, 'act_scale': act_scale}
    _L0_ffn_all = _L0_ffn_setup()
    _L0_ffn_in = {k: v for k, v in _L0_ffn_all.items() if k in ('ternary_weight', 'bias', 'act_scale')}
    del _L0_ffn_all

    def _L1_attn_setup():
        import jax, jax.numpy as jnp
        import numpy as np
        import math
        DEPTH = 12
        LAMBDA_INIT = 0.8 - 0.6 * math.exp(-0.3 * DEPTH)
        EPS = 1e-05
        key = jax.random.key(seed)
        ks = jax.random.split(key, 10)
        B, S, E, H, D = (2, 512, 256, 8, 64)
        query = jax.random.normal(ks[0], (B, S, E), dtype=jnp.float32)
        init = 0.02
        Wq = jax.random.normal(ks[1], (E, 2 * H * D), dtype=jnp.float32) * init
        Wk = jax.random.normal(ks[2], (E, 2 * H * D), dtype=jnp.float32) * init
        Wv = jax.random.normal(ks[3], (E, 2 * H * D), dtype=jnp.float32) * init
        Wo = jax.random.normal(ks[4], (2 * H * D, E), dtype=jnp.float32) * init
        lq1 = jax.random.normal(ks[5], (D,), dtype=jnp.float32) * 0.1
        lk1 = jax.random.normal(ks[6], (D,), dtype=jnp.float32) * 0.1
        lq2 = jax.random.normal(ks[7], (D,), dtype=jnp.float32) * 0.1
        lk2 = jax.random.normal(ks[8], (D,), dtype=jnp.float32) * 0.1
        subln_w = jnp.ones((2 * D,), dtype=jnp.float32)
        return {'query': query, 'Wq': Wq, 'Wk': Wk, 'Wv': Wv, 'Wo': Wo, 'lq1': lq1, 'lk1': lk1, 'lq2': lq2, 'lk2': lk2, 'subln_w': subln_w}
    _L1_attn_all = _L1_attn_setup()
    _L1_attn_in = {k: v for k, v in _L1_attn_all.items() if k in ('Wq', 'Wk', 'Wv', 'Wo', 'lq1', 'lk1', 'lq2', 'lk2', 'subln_w')}
    del _L1_attn_all

    def _L1_ffn_setup():
        import jax, jax.numpy as jnp
        import numpy as np
        B, S, D, H, E = (8, 512, 256, 1024, 16)
        key = jax.random.key(seed)
        ks = jax.random.split(key, 4)
        sd = 1.0 / np.sqrt(D).astype(np.float32)
        sh = 1.0 / np.sqrt(H).astype(np.float32)
        return {'x': jax.random.normal(ks[0], (B, S, D), jnp.float32), 'Wg': jax.random.normal(ks[1], (D, E), jnp.float32) * sd, 'bg': jnp.zeros((E,), jnp.float32), 'W1': jax.random.normal(ks[2], (E, D, H), jnp.float32) * sd, 'b1': jnp.zeros((E, H), jnp.float32), 'W2': jax.random.normal(ks[3], (E, H, D), jnp.float32) * sh, 'b2': jnp.zeros((E, D), jnp.float32)}
    _L1_ffn_all = _L1_ffn_setup()
    _L1_ffn_in = {k: v for k, v in _L1_ffn_all.items() if k in ('Wg', 'bg', 'W1', 'b1', 'W2', 'b2')}
    del _L1_ffn_all
    return {'x': x, 'L0_tok_emb_table': _L0_tok_in['emb_table'], 'L0_tok_proj_w': _L0_tok_in['proj_w'], 'L0_tok_proj_b': _L0_tok_in['proj_b'], 'L0_tok_window': _L0_tok_in['window'], 'L0_attn_w_attn': _L0_attn_in['w_attn'], 'L0_attn_w_proj': _L0_attn_in['w_proj'], 'L0_ffn_ternary_weight': _L0_ffn_in['ternary_weight'], 'L0_ffn_bias': _L0_ffn_in['bias'], 'L0_ffn_act_scale': _L0_ffn_in['act_scale'], 'L1_attn_Wq': _L1_attn_in['Wq'], 'L1_attn_Wk': _L1_attn_in['Wk'], 'L1_attn_Wv': _L1_attn_in['Wv'], 'L1_attn_Wo': _L1_attn_in['Wo'], 'L1_attn_lq1': _L1_attn_in['lq1'], 'L1_attn_lk1': _L1_attn_in['lk1'], 'L1_attn_lq2': _L1_attn_in['lq2'], 'L1_attn_lk2': _L1_attn_in['lk2'], 'L1_attn_subln_w': _L1_attn_in['subln_w'], 'L1_ffn_Wg': _L1_ffn_in['Wg'], 'L1_ffn_bg': _L1_ffn_in['bg'], 'L1_ffn_W1': _L1_ffn_in['W1'], 'L1_ffn_b1': _L1_ffn_in['b1'], 'L1_ffn_W2': _L1_ffn_in['W2'], 'L1_ffn_b2': _L1_ffn_in['b2']}

def reference(x, L0_tok_emb_table, L0_tok_proj_w, L0_tok_proj_b, L0_tok_window, L0_attn_w_attn, L0_attn_w_proj, L0_ffn_ternary_weight, L0_ffn_bias, L0_ffn_act_scale, L1_attn_Wq, L1_attn_Wk, L1_attn_Wv, L1_attn_Wo, L1_attn_lq1, L1_attn_lk1, L1_attn_lq2, L1_attn_lk2, L1_attn_subln_w, L1_ffn_Wg, L1_ffn_bg, L1_ffn_W1, L1_ffn_b1, L1_ffn_W2, L1_ffn_b2):
    import jax
    import jax.numpy as jnp

    def _L0_tok_ref(input_ids, emb_table, proj_w, proj_b, window):
        import jax, jax.numpy as jnp
        import numpy as np
        N_FFT = 64
        HOP = 64
        NUM_FREQ = N_FFT // 2 + 1

        def _stft_mag(sig, window):
            L = sig.shape[1]
            pad = N_FFT // 2
            x = jnp.pad(sig, ((0, 0), (pad, pad)), mode='reflect')
            n_frames = 1 + L // HOP
            idx = jnp.arange(n_frames)[:, None] * HOP + jnp.arange(N_FFT)[None, :]
            frames = x[:, idx] * window
            spec = jnp.fft.rfft(frames, axis=-1)
            r, im = (spec.real, spec.imag)
            m2 = r * r + im * im
            mag = jnp.where(m2 == 0, 0.0, jnp.sqrt(jnp.where(m2 == 0, 1.0, m2)))
            return (mag, n_frames)

        def _linear_interp_last(feat, out_len):
            in_len = feat.shape[-1]
            coord = jnp.clip((jnp.arange(out_len) + 0.5) * (in_len / out_len) - 0.5, 0.0, in_len - 1.0)
            i0 = jnp.floor(coord).astype(jnp.int32)
            i1 = jnp.minimum(i0 + 1, in_len - 1)
            w = (coord - i0).astype(feat.dtype)
            return feat[..., i0] * (1.0 - w) + feat[..., i1] * w
        B, L = input_ids.shape
        V = emb_table.shape[0]
        word_embeds = emb_table[input_ids]
        sig = jax.nn.one_hot(input_ids, V, dtype=jnp.float32)
        sig = jnp.transpose(sig, (0, 2, 1)).reshape(B * V, L)
        mag, T = _stft_mag(sig, window)
        feat = mag.reshape(B, V, T, NUM_FREQ).transpose(0, 3, 1, 2)
        feat = feat.reshape(B, NUM_FREQ * V, T)
        up = _linear_interp_last(feat, L)
        stft_feat = jnp.transpose(up, (0, 2, 1))
        stft_enc = stft_feat @ proj_w.T + proj_b
        return jnp.concatenate([word_embeds, stft_enc], axis=-1)

    def _L0_attn_ref(x, w_attn, w_proj):
        import jax, jax.numpy as jnp
        import numpy as np
        import math
        D = 256
        H = 16
        HEAD_D = D // H
        T = 512
        B = 4
        Bv, Tv, _ = x.shape
        qkv = x @ w_attn
        q = qkv[..., :D].reshape(Bv, Tv, H, HEAD_D).transpose(0, 2, 1, 3)
        k = qkv[..., D:D + HEAD_D]
        v = qkv[..., D + HEAD_D:]
        scale = 1.0 / math.sqrt(HEAD_D)
        att = jnp.einsum('bhqd,bkd->bhqk', q, k) * scale
        causal = jnp.tril(jnp.ones((Tv, Tv), dtype=bool))
        att = jnp.where(causal[None, None, :, :], att, -jnp.inf)
        att = jax.nn.softmax(att, axis=-1)
        y = jnp.einsum('bhqk,bkd->bhqd', att, v)
        y = y.transpose(0, 2, 1, 3).reshape(Bv, Tv, D)
        return y @ w_proj

    def _L0_ffn_ref(x, ternary_weight, bias, act_scale):
        import jax, jax.numpy as jnp
        import numpy as np
        B, S, D_IN, D_OUT = (16, 1024, 256, 256)
        ACT_BITS = 8
        QB = float(2 ** (ACT_BITS - 1) - 1)
        scale = jnp.maximum(act_scale, 1e-05)
        x_int = jnp.clip(jnp.round(x / scale), -QB, QB)
        x_dq = jnp.nan_to_num(x_int * scale, nan=0.0, posinf=10000.0, neginf=-10000.0)
        w = ternary_weight.astype(jnp.float32) - 1.0
        return jnp.einsum('bsi,oi->bso', x_dq, w) + bias

    def _L1_attn_ref(query, Wq, Wk, Wv, Wo, lq1, lk1, lq2, lk2, subln_w):
        import jax, jax.numpy as jnp
        import numpy as np
        import math
        DEPTH = 12
        LAMBDA_INIT = 0.8 - 0.6 * math.exp(-0.3 * DEPTH)
        EPS = 1e-05
        B, S, E = query.shape
        D = lq1.shape[0]
        H = Wq.shape[1] // (2 * D)
        scaling = D ** (-0.5)
        q = (query @ Wq).reshape(B, S, 2 * H, D).transpose(0, 2, 1, 3) * scaling
        k = (query @ Wk).reshape(B, S, 2 * H, D).transpose(0, 2, 1, 3)
        v = (query @ Wv).reshape(B, S, H, 2 * D).transpose(0, 2, 1, 3)
        score = jnp.einsum('bhqd,bhkd->bhqk', q, k)
        score = jnp.nan_to_num(score)
        score = jax.nn.softmax(score.astype(jnp.float32), axis=-1).astype(score.dtype)
        lambda_1 = jnp.exp(jnp.sum(lq1 * lk1))
        lambda_2 = jnp.exp(jnp.sum(lq2 * lk2))
        lambda_full = lambda_1 - lambda_2 + LAMBDA_INIT
        score = score.reshape(B, H, 2, S, S)
        score = score[:, :, 0] - lambda_full * score[:, :, 1]
        attn = jnp.einsum('bhqk,bhkd->bhqd', score, v)
        af = attn.astype(jnp.float32)
        attn = (af * jax.lax.rsqrt(jnp.mean(af * af, axis=-1, keepdims=True) + EPS)).astype(attn.dtype)
        attn = attn * subln_w
        attn = attn * (1.0 - LAMBDA_INIT)
        attn = attn.transpose(0, 2, 1, 3).reshape(B, S, H * 2 * D)
        return attn @ Wo

    def _L1_ffn_ref(x, Wg, bg, W1, b1, W2, b2):
        import jax, jax.numpy as jnp
        import numpy as np
        B, S, D, H, E = (8, 512, 256, 1024, 16)
        d = x.shape[-1]
        xf = x.reshape(-1, d)
        n_tok = xf.shape[0]
        n_exp = Wg.shape[1]
        cap = -(-n_tok // n_exp)
        score = jax.nn.softmax(xf @ Wg + bg, axis=-1)
        gate = jnp.max(score, axis=-1)
        idx = jnp.argmax(score, axis=-1)
        onehot = jax.nn.one_hot(idx, n_exp, dtype=jnp.int32)
        pos = jnp.sum((jnp.cumsum(onehot, axis=0) - 1) * onehot, axis=-1)
        keep = pos < cap
        safe_pos = jnp.where(keep, pos, cap - 1)
        buf = jnp.zeros((n_exp, cap, d), x.dtype).at[idx, safe_pos].add(jnp.where(keep[:, None], xf, 0.0))
        h = jax.nn.relu(jnp.einsum('ecd,edh->ech', buf, W1) + b1[:, None, :])
        y = jnp.einsum('ech,ehd->ecd', h, W2) + b2[:, None, :]
        out = y[idx, safe_pos] * gate[:, None]
        out = jnp.where(keep[:, None], out, 0.0)
        return out.reshape(x.shape)
    h = _L0_tok_ref(x, L0_tok_emb_table, L0_tok_proj_w, L0_tok_proj_b, L0_tok_window)
    h = h + _L0_attn_ref(_layernorm(h, axis=-1), L0_attn_w_attn, L0_attn_w_proj)
    h = h + _L0_ffn_ref(_layernorm(h, axis=-1), L0_ffn_ternary_weight, L0_ffn_bias, L0_ffn_act_scale)
    h = h + _L1_attn_ref(_layernorm(h, axis=-1), L1_attn_Wq, L1_attn_Wk, L1_attn_Wv, L1_attn_Wo, L1_attn_lq1, L1_attn_lk1, L1_attn_lq2, L1_attn_lk2, L1_attn_subln_w)
    h = h + _L1_ffn_ref(_layernorm(h, axis=-1), L1_ffn_Wg, L1_ffn_bg, L1_ffn_W1, L1_ffn_b1, L1_ffn_W2, L1_ffn_b2)
    return h

_drawn_inputs = setup_inputs


def setup_inputs(seed=0):
    import zlib

    import numpy as np

    out = dict(_drawn_inputs(seed))
    spreads = {'L0_tok_proj_b': (0.0, 0.1),
     'L1_attn_subln_w': (1.0, 0.6),
     'L1_ffn_bg': (0.0, 0.8),
     'L1_ffn_b1': (0.0, 0.8),
     'L1_ffn_b2': (0.0, 2.0)}
    factors = {'L1_attn_Wq': 8.0,
     'L1_attn_Wk': 8.0,
     'L1_attn_Wv': 5.435,
     'L1_attn_Wo': 5.253,
     'L1_attn_lq1': 8.0,
     'L1_attn_lk1': 8.0,
     'L1_attn_lq2': 8.0,
     'L1_attn_lk2': 8.0,
     'L1_ffn_Wg': 6.101,
     'L1_ffn_W1': 7.757,
     'L1_ffn_W2': 6.331}
    for name, (base, spread) in spreads.items():
        noise = np.random.default_rng([zlib.crc32(name.encode()), seed]).standard_normal(out[name].shape)
        drawn = base * np.exp(spread * noise) if base else spread * noise
        out[name] = jnp.asarray(drawn.astype(out[name].dtype))
    for name, factor in factors.items():
        out[name] = (out[name] * factor).astype(out[name].dtype)
    return out
```

```python
from contextlib import ExitStack

import concourse.bass as bass
from concourse import mybir

F32 = mybir.dt.float32
BF16 = mybir.dt.bfloat16
I32 = mybir.dt.int32
U32 = mybir.dt.uint32
ALU = mybir.AluOpType
ACT = mybir.ActivationFunctionType
AX = mybir.AxisListType

P = 128
NT = 64
D = 256
V = 64
NEMB = 179
NSTFT = D - NEMB
NFRAME = 3
NFREQ = 33
NREIM = 2 * NFREQ
NJ = 17
H0, HD0 = 16, 16
H1, HD1 = 8, 64
NE, HID, CAP = 16, 1024, 512
LAMBDA_INIT = 0.8 - 0.6 * 2.718281828459045 ** (-0.3 * 12)
EPS = 1e-5
ROUND = 12582912.0
MASKED = -1e30
NOWHERE = 65536.0
ROW = D + 2

C_ID, C_MASK, C_TRI, C_VOC, C_EXP, C_TOK, C_PART = 0, 128, 256, 384, 512, 528, 592
C_COLS = 593
C2_FRAME, C2_DFT, C2_COLS = 0, NFRAME * P, NFRAME * P + NREIM
STAGE = 3


def tower_kernel(nc, a, rows, out):
    with ExitStack() as ctx:
        def psum(name, shape, dt):
            return ctx.enter_context(nc.psum_tensor(name, shape, dt))

        m = {}
        m["bank"] = psum("bank", [P, 8, 512], F32)
        for name, shape, dt in (
            ("h", [P, NT, D], F32), ("c128", [P, C_COLS], F32), ("identb", [P, P], BF16), ("maskb", [P, P], BF16),
            ("halfneg", [P, 8], F32),
            ("wq1", [P, 2, 1024], F32), ("wk1", [P, 2, 1024], F32), ("wv1", [P, 2, 1024], F32),
            ("wo1", [P, 8, D], F32), ("subln", [P, 1], F32), ("lq", [P, 4, HD1], F32),
        ):
            m[name] = ctx.enter_context(nc.sbuf_tensor(name, shape, dt))
        for name in ("wq1", "wk1", "wv1", "wo1", "subln", "lq"):
            m["ld_" + name] = ctx.enter_context(nc.semaphore("ld_" + name))
        m["scattered"] = [ctx.enter_context(nc.semaphore(f"scattered_{i}")) for i in range(2)]
        m["prefilled"] = ctx.enter_context(nc.semaphore("prefilled"))
        m["s_out"] = ctx.enter_context(nc.semaphore("s_out"))
        token_phase(nc, a, m)
        if STAGE >= 1:
            layer0_phase(nc, a, m)
        if STAGE >= 2:
            layer1_phase(nc, a, m, rows, out)
        if STAGE >= 3:
            expert_phase(nc, a, m, rows, out)
        if STAGE < 3:
            with nc.Block() as block:
                @block.sync
                def _(sp):
                    if STAGE == 2:
                        sp.wait_ge(m["prefilled"], 16 * NT)
                        sp.wait_ge(m["scattered"][0], 16 * NT // 2)
                        sp.wait_ge(m["scattered"][1], 16 * NT // 2)
                    sp.dma_start(out.rearrange("(t p) d -> p t d", p=P), m["h"][:, :, :]).then_inc(m["s_out"], 16)
                    sp.wait_ge(m["s_out"], 16)


def token_phase(nc, a, m):
    bank, h, c128 = m["bank"], m["h"], m["c128"]
    with ExitStack() as ctx:
        def sb(name, shape, dt=F32):
            return ctx.enter_context(nc.sbuf_tensor(name, shape, dt))

        m["used_sems"] = used = []

        def sem(name):
            used.append(ctx.enter_context(nc.semaphore(name)))
            return used[-1]

        c64 = sb("c64", [V, C2_COLS])
        interp = sb("interp", [NFRAME + 1, P])
        ids_row = sb("ids_row", [V, NT * P], I32)
        ids_i = sb("ids_i", [NT, P], I32)
        ids_f = sb("ids_f", [NT, P])
        ids_col = sb("ids_col", [P, NT])
        window = sb("window", [V, 1])
        emb = sb("emb", [V, NEMB])
        projraw = sb("projraw", [NSTFT, NFREQ * V])
        projw = sb("projw", [P, NJ, NSTFT])
        wdft = sb("wdft", [V, NREIM])
        dft = sb("dft", [P, NFRAME * NREIM])
        hot = sb("hot", [P, 2, 2, P])
        square = sb("square", [P, 2, 2, NFRAME, NREIM])
        mag = sb("mag", [P, NJ, NFRAME, NT])
        spec = sb("spec", [NT, NFRAME * NSTFT])
        specrow = sb("specrow", [NFRAME + 1, NT, NSTFT])
        mag_dummy = sb("mag_dummy", [P, 3])
        hot_t = sb("hot_t", [V, 2, 2, P])

        ld_c128, ld_c64, ld_ids, ld_window = sem("t_ld_c128"), sem("t_ld_c64"), sem("t_ld_ids"), sem("t_ld_window")
        ld_row, ld_emb, ld_proj = sem("t_ld_row"), sem("t_ld_emb"), sem("t_ld_proj")
        ld_interp, ld_bias, ld_spec = sem("t_ld_interp"), sem("t_ld_bias"), sem("t_ld_spec")
        ids_ready, wdft_ready, setup_pe, dft_ready = sem("t_ids_ready"), sem("t_wdft"), sem("t_setup_pe"), sem("t_dft")
        projw_ready, mag_clear, idcol_ready = sem("t_projw"), sem("t_magclear"), sem("t_idcol")
        hot_ready, dft_done, squared, summed = sem("t_hot"), sem("t_dftdone"), sem("t_squared"), sem("t_summed")
        rooted, spec_done, spec_ready = sem("t_rooted"), sem("t_specdone"), sem("t_spec")
        hot_t_ready, tok_done, tok_stored = sem("t_hott"), sem("t_tokdone"), sem("t_tokstored")

        dft_v = dft[:, :]
        with nc.Block() as block:
            @block.sync
            def _(sp):
                sp.dma_start(c128[:, :], a["c_128"]).then_inc(ld_c128, 16)
                sp.dma_start(c64[:, :], a["c_64"]).then_inc(ld_c64, 16)
                sp.dma_start(window[:, :], a["L0_tok_window"].unsqueeze(1)).then_inc(ld_window, 16)
                sp.dma_start(ids_i[:, :], a["x"]).then_inc(ld_ids, 16)
                sp.dma_start(projraw[:, :], a["L0_tok_proj_w"]).then_inc(ld_proj, 16)
                sp.dma_start(ids_row[:, :], a["x"].rearrange("b l -> (b l)").unsqueeze(0).to_broadcast([V, NT * P]))\
                  .then_inc(ld_row, 16)
                sp.dma_start(emb[:, :], a["L0_tok_emb_table"]).then_inc(ld_emb, 16)
                sp.dma_start(interp[:, :], a["c_interp"]).then_inc(ld_interp, 16)
                sp.dma_start(specrow[NFRAME:NFRAME + 1, :, :],
                             a["L0_tok_proj_b"].unsqueeze(0).unsqueeze(0).to_broadcast([1, NT, NSTFT]))\
                  .then_inc(ld_bias, 16)
                sp.wait_ge(spec_ready, 1)
                for t in range(NFRAME):
                    sp.dma_start(specrow[t:t + 1, :, :], spec[:, t * NSTFT:(t + 1) * NSTFT]).then_inc(ld_spec, 16)

            @block.gpsimd
            def _(pool):
                nc.gpsimd.memset(mag[:, :, :, :], 0.0).then_inc(mag_clear, 1)
                nc.gpsimd.memset(mag_dummy[:, 0:1], 0.0).then_inc(squared, 2)
                nc.gpsimd.memset(mag_dummy[:, 1:2], 0.0).then_inc(summed, 2)
                nc.gpsimd.memset(mag_dummy[:, 2:3], 0.0).then_inc(tok_stored, 2)
                nc.gpsimd.memset(m["halfneg"][:, :], -0.5).then_inc(mag_clear, 1)

            @block.tensor
            def _(pe):
                pe.wait_ge(wdft_ready, 1)
                for t in range(NFRAME):
                    mm = nc.tensor.matmul(bank[:, 0, t * NREIM:(t + 1) * NREIM], c64[:, C2_FRAME + P * t:C2_FRAME + P * (t + 1)],
                                          wdft[:, :], start=True, stop=True)
                mm.then_inc(setup_pe, 1)
                pe.wait_ge(ids_ready, 1)
                nc.tensor.transpose(bank[:, 1, 0:NT], ids_f[:, :], c128[0:NT, C_ID:C_ID + NT]).then_inc(setup_pe, 1)
                pe.wait_ge(ld_proj, 16)
                for j in range(NJ):
                    w = P if j < NJ - 1 else V
                    at = (j % 6) * NSTFT
                    mm = nc.tensor.transpose(bank[0:w, 2 + j // 6, at:at + NSTFT], projraw[:, P * j:P * j + w],
                                             c128[0:NSTFT, C_ID:C_ID + NSTFT])
                mm.then_inc(setup_pe, 1)
                pe.wait_ge(dft_ready, 1)
                with pe.Fori(0, NT // 4) as i:
                    for p in range(2):
                        n = 2 * i + p
                        pe.wait_ge(hot_ready, n + 1)
                        pe.wait_ge(squared, n + 1)
                        for b in range(2):
                            mm = nc.tensor.matmul(bank[:, 5 + p, b * 198:(b + 1) * 198], hot[:, p, b, :], dft_v,
                                                  start=True, stop=True)
                        mm.then_inc(dft_done, 1)
                pe.wait_ge(rooted, 1)
                pe.wait_ge(projw_ready, 1)
                for t in range(NFRAME):
                    for j in range(NJ):
                        w = P if j < NJ - 1 else V
                        mm = nc.tensor.matmul(bank[0:NT, 7, t * NSTFT:(t + 1) * NSTFT], mag[0:w, j, t, :],
                                              projw[0:w, j, :], start=(j == 0), stop=(j == NJ - 1))
                mm.then_inc(spec_done, 1)
                pe.wait_ge(ld_emb, 16)
                pe.wait_ge(ld_interp, 16)
                pe.wait_ge(ld_bias, 16)
                pe.wait_ge(ld_spec, 16 * NFRAME)
                with pe.Fori(0, NT // 4) as i:
                    for p in range(2):
                        n = 2 * i + p
                        pe.wait_ge(hot_t_ready, n + 1)
                        pe.wait_ge(tok_stored, n + 1)
                        for b in range(2):
                            nc.tensor.matmul(bank[:, p, b * D:b * D + NEMB], hot_t[:, p, b, :], emb[:, :],
                                             start=True, stop=True)
                            mm = nc.tensor.matmul(bank[:, p, b * D + NEMB:(b + 1) * D], interp[:, :],
                                                  specrow[:, 2 * n + b, :], start=True, stop=True)
                        mm.then_inc(tok_done, 1)

            @block.vector
            def _(dve):
                dve.wait_ge(ld_ids, 16)
                nc.vector.tensor_copy(ids_f[:, :], ids_i[:, :]).then_inc(ids_ready, 1)
                dve.wait_ge(ld_c128, 16)
                nc.vector.tensor_copy(m["identb"][:, :], c128[:, C_ID:C_ID + P])
                nc.vector.tensor_copy(m["maskb"][:, :], c128[:, C_MASK:C_MASK + P])
                dve.wait_ge(ld_c64, 16)
                dve.wait_ge(ld_window, 16)
                nc.vector.tensor_scalar(wdft[:, :], c64[:, C2_DFT:C2_DFT + NREIM], window[:, 0:1], None, ALU.mult)\
                  .then_inc(wdft_ready, 1)
                dve.wait_ge(setup_pe, 1)
                nc.vector.tensor_copy(dft[:, :], bank[:, 0, 0:NFRAME * NREIM]).then_inc(dft_ready, 1)
                dve.wait_ge(setup_pe, 2)
                nc.vector.tensor_copy(ids_col[:, :], bank[:, 1, 0:NT]).then_inc(idcol_ready, 1)
                dve.wait_ge(setup_pe, 3)
                nc.vector.tensor_copy(projw[:, 0:6, :], bank[:, 2, 0:6 * NSTFT].rearrange("p (j o) -> p j o", j=6))
                nc.vector.tensor_copy(projw[:, 6:12, :], bank[:, 3, 0:6 * NSTFT].rearrange("p (j o) -> p j o", j=6))
                nc.vector.tensor_copy(projw[:, 12:16, :], bank[:, 4, 0:4 * NSTFT].rearrange("p (j o) -> p j o", j=4))
                nc.vector.tensor_copy(projw[0:V, 16, :], bank[0:V, 4, 4 * NSTFT:5 * NSTFT]).then_inc(projw_ready, 1)
                dve.wait_ge(mag_clear, 2)

                def one_hots(n, p):
                    nc.vector.tensor_tensor(
                        hot[:, p], c128[:, C_VOC:C_VOC + P].unsqueeze(1).to_broadcast([P, 2, P]),
                        ids_col[:, bass.ds(2 * n, 2)].unsqueeze(2).to_broadcast([P, 2, P]), ALU.is_equal)\
                      .then_inc(hot_ready, 1)

                def powers(i, more):
                    for p in range(2):
                        n = 2 * i + p
                        dve.wait_ge(squared, n + 3)
                        for half in range(2):
                            lo, k = half * V, NJ - half
                            s = square[lo:lo + V, p]
                            mm = nc.vector.tensor_tensor(
                                mag[lo:lo + V, 0:k, :, bass.ds(2 * n, 2)].rearrange("p j t b -> p b t j"),
                                s[:, :, :, half:NFREQ:2], s[:, :, :, NFREQ + half:NREIM:2], ALU.add)
                        mm.then_inc(summed, 1)
                        if more:
                            one_hots(n + 2, p)

                dve.wait_ge(idcol_ready, 1)
                one_hots(0, 0)
                one_hots(1, 1)
                with dve.Fori(0, NT // 4 - 1) as i:
                    powers(i, True)
                powers(NT // 4 - 1, False)
                dve.wait_ge(spec_done, 1)
                nc.vector.tensor_copy(spec[:, :], bank[0:NT, 7, 0:NFRAME * NSTFT]).then_inc(spec_ready, 1)
                dve.wait_ge(ld_row, 16)
                with dve.Fori(0, NT // 4) as i:
                    for p in range(2):
                        n = 2 * i + p
                        dve.wait_ge(tok_stored, n + 1)
                        nc.vector.tensor_scalar(hot_t[:, p], ids_row[:, bass.ds(2 * P * n, 2 * P)]
                                                .rearrange("p (b l) -> p b l", b=2), c128[0:V, C_PART:C_PART + 1], None,
                                                ALU.is_equal).then_inc(hot_t_ready, 1)

            @block.scalar
            def _(act):
                for k, name in (("wq1", "L1_attn_Wq"), ("wk1", "L1_attn_Wk"), ("wv1", "L1_attn_Wv")):
                    act.dma_start(m[k][:, :, :], a[name].rearrange("(k p) n -> p k n", p=P)).then_inc(m["ld_" + k], 16)
                act.dma_start(m["wo1"][:, :, :], a["L1_attn_Wo"].rearrange("(n p) d -> p n d", p=P)).then_inc(m["ld_wo1"], 16)
                act.dma_start(m["subln"][:, :], a["L1_attn_subln_w"].unsqueeze(1)).then_inc(m["ld_subln"], 16)
                for k, name in enumerate(("L1_attn_lq1", "L1_attn_lk1", "L1_attn_lq2", "L1_attn_lk2")):
                    act.dma_start(m["lq"][:, k, :], a[name].unsqueeze(0).to_broadcast([P, HD1])).then_inc(m["ld_lq"], 16)
                nc.scalar.preload_act_table(ACT.Sqrt)
                with act.Fori(0, NT // 4) as i:
                    for p in range(2):
                        n = 2 * i + p
                        act.wait_ge(dft_done, n + 1)
                        act.wait_ge(summed, n + 1)
                        nc.scalar.activation(square[:, p].rearrange("p b t c -> p (b t c)"), bank[:, 5 + p, 0:396],
                                             ACT.Square).then_inc(squared, 1)
                act.wait_ge(summed, NT // 2 + 2)
                for j in range(NJ):
                    mm = nc.scalar.activation(mag[:, j], mag[:, j], ACT.Sqrt)
                mm.then_inc(rooted, 1)
                with act.Fori(0, NT // 4) as i:
                    for p in range(2):
                        n = 2 * i + p
                        act.wait_ge(tok_done, n + 1)
                        nc.scalar.copy(h[:, bass.ds(2 * n, 2), :], bank[:, p, :].rearrange("p (b d) -> p b d", b=2))\
                          .then_inc(tok_stored, 1)


def layer0_phase(nc, a, m):
    bank, h, c128 = m["bank"], m["h"], m["c128"]
    ident = c128[:, C_ID:C_ID + P]
    spent = [s.num for s in m["used_sems"]]
    with ExitStack() as ctx:
        def sb(name, shape, dt=F32):
            return ctx.enter_context(nc.sbuf_tensor(name, shape, dt))

        m["used_sems"] = used = []

        def sem(name):
            used.append(ctx.enter_context(nc.semaphore(name)))
            return used[-1]

        w_raw = sb("w_raw", [P, 2, D + 2 * HD0])
        wq = sb("wq", [P, 2, 4, P])
        wk = sb("wk", [P, 2, P])
        wp = sb("wp", [P, 2, D])
        tern_i = sb("tern_i", [P, 2, D], I32)
        tern = sb("tern", [P, 2, D], BF16)
        wt = sb("wt", [P, 2, D], BF16)
        bias = sb("bias0", [P, D])
        scale = sb("scale0", [P, 1])
        rscale = sb("rscale", [P, 1])
        stats = sb("stats", [P, 2, 6])
        meanvar = sb("meanvar", [P, 2, 2])
        rstd = sb("rstd", [P, 2])
        xn = sb("xn", [P, 2, D])
        xnT = sb("xnT", [P, 2, 2, P])
        qT = sb("qT", [P, 2, 4, P])
        kT = sb("kT", [P, 2, P])
        vone = sb("vone", [P, 2, HD0 + 1])
        negmax = sb("negmax", [P, 4, 4])
        prob = sb("prob", [P, 4, 4, P])
        probT = sb("probT", [P, 2, 4, P])
        rsum = sb("rsum", [P, H0])
        att = sb("att", [P, 2, D])
        attT = sb("attT", [P, 2, 2, P])
        stats2 = sb("stats2", [P, 6])
        meanvar2 = sb("meanvar2", [P, 2])
        rstd2 = sb("rstd2", [P, 1])
        rq = sb("rq", [P, 1])
        xq = sb("xq", [P, D])
        xc = sb("xc", [P, D])
        xi = sb("xi", [P, 2, D], BF16)
        xiT = sb("xiT", [P, 2, 2, P], BF16)

        ld_w, ld_wp, ld_t, ld_b, ld_s = sem("z_ld_w"), sem("z_ld_wp"), sem("z_ld_t"), sem("z_ld_b"), sem("z_ld_s")
        cleared, weights, tern_ready, tern_turned, setup = \
            sem("z_cleared"), sem("z_weights"), sem("z_tern"), sem("z_ternT"), sem("z_setup")
        s_mean, s_rstd, s_xn, s_xnT_ps, s_xnT = \
            sem("z_mean"), sem("z_rstd"), sem("z_xn"), sem("z_xnT_ps"), sem("z_xnT")
        s_q_ps, s_q, s_kv_ps, s_kv = sem("z_q_ps"), sem("z_q"), sem("z_kv_ps"), sem("z_kv")
        s_score, s_max, s_prob, s_pT_ps, s_pT, s_pv = \
            sem("z_score"), sem("z_max"), sem("z_prob"), sem("z_pT_ps"), sem("z_pT"), sem("z_pv")
        s_rsum, s_att, s_aT_ps, s_aT, s_proj, s_res = \
            sem("z_rsum"), sem("z_att"), sem("z_aT_ps"), sem("z_aT"), sem("z_proj"), sem("z_res")
        s_stat, s_stat2, s_mean2, s_rstd2, s_rq, s_xq, s_xc, s_xi = \
            sem("z_stat"), sem("z_stat2"), sem("z_mean2"), sem("z_rstd2"), sem("z_rq"), sem("z_xq"), sem("z_xc"), sem("z_xi")
        s_xiT_ps, s_xiT, s_ffn, s_bias, s_var, s_var2, s_done = \
            sem("z_xiT_ps"), sem("z_xiT"), sem("z_ffn"), sem("z_bias"), sem("z_var"), sem("z_var2"), sem("z_done")

        BT, BF, BO, BM = 4, 5, 6, 7

        def steps(step, engine):
            def peeled(t):
                step(t, t % 2, lambda lag: 0 <= t - lag < NT)

            for t in range(-2, 4):
                peeled(t)
            with engine.Fori(0, (NT - 6) // 2) as i:
                for p in range(2):
                    step(2 * i + (4 + p), p, lambda lag: True)
            for t in range(NT - 2, NT + 3):
                peeled(t)

        with nc.Block() as block:
            @block.sync
            def _(sp):
                sp.dma_start(w_raw[:, :, :], a["L0_attn_w_attn"].rearrange("(k p) n -> p k n", p=P)).then_inc(ld_w, 16)
                sp.dma_start(tern_i[:, :, :], a["L0_ffn_ternary_weight"].rearrange("(k p) n -> p k n", p=P))\
                  .then_inc(ld_t, 16)
                sp.dma_start(scale[:, :], a["L0_ffn_act_scale"].unsqueeze(0).to_broadcast([P, 1])).then_inc(ld_s, 16)
                sp.dma_start(wp[:, :, :], a["L0_attn_w_proj"].rearrange("(k p) n -> p k n", p=P)).then_inc(ld_wp, 16)
                sp.dma_start(bias[:, :], a["L0_ffn_bias"].unsqueeze(0).to_broadcast([P, D])).then_inc(ld_b, 16)

            @block.gpsimd
            def _(pool):
                nc.gpsimd.sem_clear(range(min(spent), max(spent) + 1))
                nc.gpsimd.memset(wq[:, :, :, :], 0.0)
                nc.gpsimd.memset(wk[:, :, :], 0.0)
                nc.gpsimd.memset(vone[:, :, :], 1.0).then_inc(cleared, 1)
                pool.wait_ge(ld_b, 16)

                def step(t, p, has):
                    if has(-2):
                        pool.wait_ge(s_var, t + 3)
                        nc.gpsimd.tensor_tensor(rstd[:, p:p + 1], rstd[:, p:p + 1], m["halfneg"][:, 0:1], ALU.pow)\
                          .then_inc(s_rstd, 1)
                    if has(2):
                        pool.wait_ge(s_var2, t - 1)
                        nc.gpsimd.tensor_tensor(rstd2[:, :], rstd2[:, :], m["halfneg"][:, 0:1], ALU.pow)\
                          .then_inc(s_rstd2, 1)
                        pool.wait_ge(s_xq, t - 1)
                        nc.gpsimd.tensor_tensor(h[:, bass.ds(t - 2, 1), :].squeeze(1), h[:, bass.ds(t - 2, 1), :].squeeze(1),
                                                bias[:, :], ALU.add).then_inc(s_bias, 1)

                steps(step, pool)

            @block.tensor
            def _(pe):
                pe.wait_ge(tern_ready, 1)
                for o in range(2):
                    for i in range(2):
                        mm = nc.tensor.transpose(bank[:, BF, 64 * (2 * i + o):64 * (2 * i + o + 1)].bitcast(BF16),
                                                 tern[:, o, i * P:(i + 1) * P], m["identb"][:, :])
                mm.then_inc(tern_turned, 1)
                pe.wait_ge(setup, 1)
                pe.wait_ge(ld_wp, 16)

                def step(t, p, has):
                    q = 1 - p
                    for u in range(4):
                        if has(0):
                            if u == 0:
                                pe.wait_ge(s_q, t + 1)
                                pe.wait_ge(s_kv, t + 1)
                            if has(1):
                                pe.wait_ge(s_prob, 4 * t + u - 3)
                            nc.tensor.matmul(bank[:, u, :].rearrange("p (c k) -> p c k", c=4), m["identb"][:, :],
                                             m["maskb"][:, :].unsqueeze(1).to_broadcast([P, 4, P]),
                                             start=True, stop=False, skip_group_check=True)
                            for c in range(4):
                                mm = nc.tensor.matmul(bank[:, u, c * P:(c + 1) * P], qT[32 * u:32 * u + HD0, p, c, :],
                                                      kT[32 * u:32 * u + HD0, p, :], start=False, stop=(c == 3),
                                                      skip_group_check=True)
                            mm.then_inc(s_score, 1)
                        if has(0) if u >= 2 else has(1):
                            v = (u + 2) % 4
                            n = 4 * t + u - 2
                            pe.wait_ge(s_prob, n + 1)
                            if not (u == 2 and not has(1)):
                                pe.wait_ge(s_pT, n)
                            for c in range(4):
                                mm = nc.tensor.transpose(bank[:, BT, c * P:(c + 1) * P], prob[:, v, c, :], ident)
                            mm.then_inc(s_pT_ps, 1)
                        if has(0) if u >= 3 else has(1):
                            v = (u + 1) % 4
                            n = 4 * t + u - 3
                            pv = p if u == 3 else q
                            pe.wait_ge(s_pT, n + 1)
                            if u == 3 and has(1):
                                pe.wait_ge(s_att, t)
                            for c in range(4):
                                at = (4 * c + v) * (HD0 + 1)
                                mm = nc.tensor.matmul(bank[:, BO, at:at + HD0 + 1], probT[:, v % 2, c, :], vone[:, pv, :],
                                                      start=True, stop=True)
                            mm.then_inc(s_pv, 1)
                        if u == 0:
                            if has(-1):
                                pe.wait_ge(s_xn, t + 2)
                                if has(0):
                                    pe.wait_ge(s_q, t + 1)
                                for k in range(2):
                                    mm = nc.tensor.transpose(bank[:, BF, k * P:(k + 1) * P], xn[:, q, k * P:(k + 1) * P], ident)
                                mm.then_inc(s_xnT_ps, 1)
                            if has(3):
                                pe.wait_ge(s_xi, t - 2)
                                if not has(-1):
                                    pe.wait_ge(s_xiT, t - 3)
                                for k in range(2):
                                    mm = nc.tensor.transpose(bank[:, BF, D + 64 * k:D + 64 * (k + 1)].bitcast(BF16),
                                                             xi[:, q, k * P:(k + 1) * P], m["identb"][:, :])
                                mm.then_inc(s_xiT_ps, 1)
                            if has(2):
                                pe.wait_ge(s_att, t - 1)
                                if has(-0):
                                    pe.wait_ge(s_kv, t + 1)
                                if has(4):
                                    pe.wait_ge(s_done, t - 3)
                                for k in range(2):
                                    mm = nc.tensor.transpose(bank[:, BM, k * P:(k + 1) * P], att[:, p, k * P:(k + 1) * P], ident)
                                mm.then_inc(s_aT_ps, 1)
                        if u == 1 and has(2):
                            pe.wait_ge(s_aT, t - 1)
                            for k in range(2):
                                mm = nc.tensor.matmul(bank[:, BM, 0:D], attT[:, p, k, :], wp[:, k, :],
                                                      start=(k == 0), stop=(k == 1))
                            mm.then_inc(s_proj, 1)
                        if u == 2:
                            if has(-1):
                                pe.wait_ge(s_xnT, t + 2)
                                if has(3):
                                    pe.wait_ge(s_xiT, t - 2)
                                for c in range(4):
                                    for k in range(2):
                                        mm = nc.tensor.matmul(bank[:, BF, c * P:(c + 1) * P], wq[:, k, c, :], xnT[:, q, k, :],
                                                              start=(k == 0), stop=(k == 1))
                                mm.then_inc(s_q_ps, 1)
                            if has(2):
                                pe.wait_ge(s_res, t - 1)
                            if has(-1):
                                for k in range(2):
                                    nc.tensor.matmul(bank[:, BM, 0:P], wk[:, k, :], xnT[:, q, k, :],
                                                     start=(k == 0), stop=(k == 1))
                                for k in range(2):
                                    mm = nc.tensor.matmul(bank[:, BM, P:P + HD0], xnT[:, q, k, :],
                                                          w_raw[:, k, D + HD0:D + 2 * HD0], start=(k == 0), stop=(k == 1))
                                mm.then_inc(s_kv_ps, 1)
                            if has(3):
                                pe.wait_ge(s_xiT, t - 2)
                                for k in range(2):
                                    mm = nc.tensor.matmul(bank[:, BM, D:2 * D], xiT[:, q, k, :], wt[:, k, :],
                                                          start=(k == 0), stop=(k == 1))
                                mm.then_inc(s_ffn, 1)

                steps(step, pe)

            @block.vector
            def _(dve):
                dve.wait_ge(ld_t, 16)
                nc.vector.tensor_scalar(tern[:, :, :], tern_i[:, :, :], -1.0, None, ALU.add).then_inc(tern_ready, 1)
                dve.wait_ge(cleared, 1)
                dve.wait_ge(ld_w, 16)
                for k in range(2):
                    for c in range(4):
                        nc.vector.tensor_scalar(
                            wq[:, k, c, :].rearrange("p (r d) -> p r d", r=4)[:, :, 0:HD0],
                            w_raw[:, k, 4 * c * HD0:4 * (c + 1) * HD0].rearrange("p (r d) -> p r d", r=4),
                            HD0 ** -0.5, None, ALU.mult)
                    for r in range(4):
                        nc.vector.tensor_copy(wk[:, k, 32 * r:32 * r + HD0], w_raw[:, k, D:D + HD0])
                dve.wait_ge(ld_s, 16)
                nc.vector.tensor_scalar(scale[:, :], scale[:, :], 1e-5, 3e38, ALU.max, ALU.min).then_inc(weights, 1)
                dve.wait_ge(weights, 1)
                nc.vector.reciprocal(rscale[:, :], scale[:, :])
                dve.wait_ge(tern_turned, 1)
                nc.vector.tensor_copy(wt[:, :, :], bank[:, BF, 0:256].bitcast(BF16).rearrange("p (k n) -> p k n", k=2))\
                  .then_inc(setup, 1)

                def step(t, p, has):
                    q = 1 - p
                    for u in range(4):
                        if u == 1 and has(-2):
                            dve.wait_ge(s_stat, t + 3)
                        if has(0):
                            dve.wait_ge(s_score, 4 * t + u + 1)
                            nc.vector.tensor_reduce(negmax[:, u, :], bank[:, u, :].rearrange("p (c k) -> p c k", c=4),
                                                    AX.X, ALU.max, negate=True).then_inc(s_max, 1)
                        if u == 0:
                            if has(2):
                                dve.wait_ge(s_aT_ps, t - 1)
                                nc.vector.tensor_copy(attT[:, p], bank[:, BM, 0:D].rearrange("p (k n) -> p k n", k=2))\
                                  .then_inc(s_aT, 1)
                            if has(-2):
                                nc.vector.bn_stats(stats[:, p, :], h[:, bass.ds(t + 2, 1), :].squeeze(1)).then_inc(s_stat, 1)
                        if u == 1:
                            if has(-2):
                                nc.vector.bn_aggr(meanvar[:, p, :], stats[:, p, :]).then_inc(s_mean, 1)
                                dve.wait_ge(s_mean, t + 3)
                                nc.vector.tensor_scalar(rstd[:, p:p + 1], meanvar[:, p, 1:2], EPS, None, ALU.add)\
                                  .then_inc(s_var, 1)
                            if has(-1):
                                dve.wait_ge(s_xnT_ps, t + 2)
                                nc.vector.tensor_copy(xnT[:, q], bank[:, BF, 0:D].rearrange("p (k n) -> p k n", k=2))\
                                  .then_inc(s_xnT, 1)
                            if has(3):
                                dve.wait_ge(s_xiT_ps, t - 2)
                                nc.vector.tensor_copy(xiT[:, q], bank[:, BF, D:D + P].bitcast(BF16)
                                                      .rearrange("p (k n) -> p k n", k=2)).then_inc(s_xiT, 1)
                        if u == 2:
                            o = bank[:, BO, 0:H0 * (HD0 + 1)].rearrange("p (n d) -> p n d", n=H0)
                            if has(2):
                                dve.wait_ge(s_proj, t - 1)
                                ht = h[:, bass.ds(t - 2, 1), :].squeeze(1)
                                nc.vector.tensor_tensor(ht, ht, bank[:, BM, 0:D], ALU.add).then_inc(s_res, 1)
                                dve.wait_ge(s_res, t - 1)
                            if has(1):
                                dve.wait_ge(s_pv, 4 * t)
                                nc.vector.reciprocal(rsum[:, :], o[:, :, HD0]).then_inc(s_rsum, 1)
                            if has(2):
                                nc.vector.bn_stats(stats2[:, :], ht).then_inc(s_stat2, 1)
                                dve.wait_ge(s_stat2, t - 1)
                            if has(1):
                                dve.wait_ge(s_rsum, t)
                                nc.vector.tensor_tensor(att[:, q].rearrange("p (n d) -> p n d", n=H0), o[:, :, 0:HD0],
                                                        rsum[:, :].unsqueeze(2).to_broadcast([P, H0, HD0]), ALU.mult)\
                                  .then_inc(s_att, 1)
                            if has(2):
                                nc.vector.bn_aggr(meanvar2[:, :], stats2[:, :]).then_inc(s_mean2, 1)
                                dve.wait_ge(s_mean2, t - 1)
                                nc.vector.tensor_scalar(rstd2[:, :], meanvar2[:, 1:2], EPS, None, ALU.add).then_inc(s_var2, 1)
                        if u == 3:
                            if has(-1):
                                dve.wait_ge(s_kv_ps, t + 2)
                                nc.vector.tensor_copy(kT[:, q], bank[:, BM, 0:P])
                                nc.vector.tensor_copy(vone[:, q, 0:HD0], bank[:, BM, P:P + HD0]).then_inc(s_kv, 1)
                            if has(3):
                                dve.wait_ge(s_ffn, t - 2)
                                dve.wait_ge(s_bias, t - 2)
                                ht = h[:, bass.ds(t - 3, 1), :].squeeze(1)
                                nc.vector.scalar_tensor_tensor(out=ht, in0=bank[:, BM, D:2 * D], scalar=scale[:, 0:1],
                                                               in1=ht, op0=ALU.mult, op1=ALU.add).then_inc(s_done, 1)
                            if has(-2):
                                dve.wait_ge(s_rstd, t + 3)
                                nc.vector.tensor_scalar(xn[:, p], h[:, bass.ds(t + 2, 1), :].squeeze(1),
                                                        meanvar[:, p, 0:1], rstd[:, p:p + 1], ALU.subtract, ALU.mult)\
                                  .then_inc(s_xn, 1)
                            if has(2):
                                dve.wait_ge(s_rstd2, t - 1)
                                nc.vector.tensor_scalar(xq[:, :], h[:, bass.ds(t - 2, 1), :].squeeze(1),
                                                        meanvar2[:, 0:1], rstd2[:, 0:1], ALU.subtract, ALU.mult)\
                                  .then_inc(s_xq, 1)
                                dve.wait_ge(s_xq, t - 1)
                                nc.vector.tensor_scalar(xc[:, :], xq[:, :], rscale[:, 0:1], 127.0, ALU.mult, ALU.min)\
                                  .then_inc(s_xc, 1)
                                dve.wait_ge(s_xc, t - 1)
                                nc.vector.tensor_scalar(xq[:, :], xc[:, :], -127.0, ROUND, ALU.max, ALU.add).then_inc(s_rq, 1)
                                dve.wait_ge(s_rq, t - 1)
                                nc.vector.tensor_scalar(xi[:, p], xq[:, :], -ROUND, None, ALU.add).then_inc(s_xi, 1)

                steps(step, dve)

            @block.scalar
            def _(act):
                nc.scalar.preload_act_table(ACT.Exp)

                def step(t, p, has):
                    q = 1 - p
                    for u in range(4):
                        if u == 3 and has(-1):
                            act.wait_ge(s_q_ps, t + 2)
                            nc.scalar.copy(qT[:, q], bank[:, BF, :].rearrange("p (c n) -> p c n", c=4)).then_inc(s_q, 1)
                        if has(0):
                            act.wait_ge(s_max, 4 * t + u + 1)
                            for c in range(4):
                                mm = nc.scalar.activation(prob[:, u, c, :], bank[:, u, c * P:(c + 1) * P], ACT.Exp,
                                                          bias=negmax[:, u, c:c + 1])
                            mm.then_inc(s_prob, 1)
                        if has(0) if u >= 2 else has(1):
                            n = 4 * t + u - 2
                            act.wait_ge(s_pT_ps, n + 1)
                            nc.scalar.copy(probT[:, u % 2], bank[:, BT, :].rearrange("p (c n) -> p c n", c=4))\
                              .then_inc(s_pT, 1)

                steps(step, act)


def layer1_phase(nc, a, m, rows, out):
    bank, h, c128 = m["bank"], m["h"], m["c128"]
    ident = c128[:, C_ID:C_ID + P]
    wq, wk, wv, wo, lq = m["wq1"], m["wk1"], m["wv1"], m["wo1"], m["lq"]
    spent = [s.num for s in m["used_sems"]]
    with ExitStack() as ctx:
        def sb(name, shape, dt=F32):
            return ctx.enter_context(nc.sbuf_tensor(name, shape, dt))

        def sem(name):
            return ctx.enter_context(nc.semaphore(name))

        wg = sb("wg", [P, 2, NE])
        bg = sb("bg", [P, NE])
        ones = sb("ones", [P, P])
        blank = sb("blank", [P, ROW])
        lprod = sb("lprod", [P, 2, HD1])
        lsum = sb("lsum", [P, 2])
        lexp = sb("lexp", [P, 2])
        neglam = sb("neglam", [P, 1])
        xn = sb("xn1", [P, 2, D])
        xnT = sb("xnT1", [P, 2, 2, P])
        qT = sb("qT1", [P, 2, H1, P])
        kT = sb("kT1", [P, 2, H1, P])
        val = sb("val1", [P, 2, H1 * P])
        stats = sb("stats1", [P, 6])
        meanvar = sb("meanvar1", [P, 2])
        rstd = sb("rstd1", [P, 1])
        negmax = sb("negmax1", [P, 2, 8])
        prob = sb("prob1", [P, 2, 8, P])
        psum_ = sb("psum1", [P, 2, 8])
        rsec = sb("rsec", [P, 4])
        ratio = sb("ratio", [P, 4])
        epsum = sb("epsum", [P, 2, 4])
        diff = sb("diff", [P, 2, 4, P])
        diffT = sb("diffT", [P, 2, 4, P])
        junk = sb("junk", [P, 2, 4, P])
        ssq = sb("ssq", [P, 2, 4])
        meansq = sb("meansq", [P, 2, 4])
        normed = sb("normed", [P, 2, 4, P])
        normedT = sb("normedT", [P, 2, 4, P])
        gstats = sb("gstats", [P, 6])
        gmeanvar = sb("gmeanvar", [P, 2])
        grstd = sb("grstd", [P, 1])
        gn = sb("gn", [P, D])
        gnT = sb("gnT", [P, 2, P])
        logit = sb("logit", [P, NE])
        glmax = sb("glmax", [P, 1])
        gnegmax = sb("gnegmax", [P, 1])
        gexp = sb("gexp", [P, NE])
        gsum = sb("gsum", [P, 1])
        top = sb("top", [P, NE])
        cand = sb("cand", [P, NE])
        first = sb("first", [P, 1])
        hot = sb("hot1", [P, NE])
        hotsum = sb("hotsum", [P, NE])
        posjunk = sb("posjunk", [P, NE])
        pos = sb("pos", [P, 1])
        over = sb("over", [P, 1])
        slotf = sb("slotf", [P, 1])
        slot = sb("slot", [P, 2], U32)
        row = sb("row", [P, 2, ROW])

        ld_wg, ld_bg = sem("y_ld_wg"), sem("y_ld_bg")
        blanked, blank_ready, setup_pool, setup_dve = sem("y_blanked"), sem("y_blank"), sem("y_setup_pool"), sem("y_setup_dve")
        s_lprod, s_lsum, s_lexp, s_lam = sem("y_lprod"), sem("y_lsum"), sem("y_lexp"), sem("y_lam")
        s_stat, s_mean, s_var, s_rstd, s_xn, s_xnT_ps, s_xnT = \
            sem("y_stat"), sem("y_mean"), sem("y_var"), sem("y_rstd"), sem("y_xn"), sem("y_xnT_ps"), sem("y_xnT")
        s_fill, s_fa, s_fd = sem("y_fill"), sem("y_fill_act"), sem("y_fill_dve")
        s_score, s_max, s_exp = sem("y_score"), sem("y_max"), sem("y_exp")
        s_rsec, s_ratio, s_diff, s_dT_ps, s_dT = sem("y_rsec"), sem("y_ratio"), sem("y_diff"), sem("y_dT_ps"), sem("y_dT")
        s_pv, s_sq, s_msq, s_fac, s_norm, s_nT_ps, s_nT = \
            sem("y_pv"), sem("y_sq"), sem("y_msq"), sem("y_fac"), sem("y_norm"), sem("y_nT_ps"), sem("y_nT")
        s_eps, s_wo, s_res = sem("y_eps"), sem("y_wo"), sem("y_res")
        g_stat, g_mean, g_var, g_rstd, g_norm, g_T_ps, g_T = \
            sem("g_stat"), sem("g_mean"), sem("g_var"), sem("g_rstd"), sem("g_norm"), sem("g_T_ps"), sem("g_T")
        g_lg_ps, g_lg, g_max, g_neg, g_exp, g_gate, g_top, g_cand, g_first, g_hot = \
            sem("g_lg_ps"), sem("g_lg"), sem("g_max"), sem("g_neg"), sem("g_exp"), sem("g_gate"), sem("g_top"), \
            sem("g_cand"), sem("g_first"), sem("g_hot")
        g_ps, g_pos, g_sum, g_over, g_slotf, g_slot, g_row = \
            sem("g_ps"), sem("g_pos"), sem("g_sum"), sem("g_over"), sem("g_slotf"), sem("g_slot"), sem("g_row")

        BD, BV, BX, BP = 4, 5, 6, 7

        def steps(step, engine):
            def peeled(t):
                step(t, t % 2, lambda lag: 0 <= t - lag < NT)

            for t in range(-3, 4):
                peeled(t)
            with engine.Fori(0, (NT - 8) // 2) as i:
                for p in range(2):
                    step(2 * i + (4 + p), p, lambda lag: True)
            for t in range(NT - 4, NT + 4):
                peeled(t)

        with nc.Block() as block:
            @block.sync
            def _(sp):
                sp.dma_start(wg[:, :, :], a["L1_ffn_Wg"].rearrange("(k p) n -> p k n", p=P)).then_inc(ld_wg, 16)
                sp.dma_start(bg[:, :], a["L1_ffn_bg"].unsqueeze(0).to_broadcast([P, NE])).then_inc(ld_bg, 16)
                sp.wait_ge(blank_ready, 2)
                sp.dma_start(rows.rearrange("(s p) c -> p s c", p=P),
                             blank[:, :].unsqueeze(1).to_broadcast([P, NT, ROW])).then_inc(blanked, 16)

                def step(t, p, has):
                    if has(1):
                        sp.wait_ge(s_res, t)
                        sp.dma_start(out[bass.ds(P * (t - 1), P), :], h[:, bass.ds(t - 1, 1), :].squeeze(1))\
                          .then_inc(m["prefilled"], 16)

                steps(step, sp)

            @block.gpsimd
            def _(pool):
                nc.gpsimd.sem_clear(range(min(spent), max(spent) + 1))
                nc.gpsimd.memset(ones[:, :], 1.0)
                nc.gpsimd.memset(hotsum[:, :], 0.0).then_inc(setup_pool, 1)
                nc.gpsimd.memset(blank[:, :], 0.0).then_inc(blank_ready, 1)
                pool.wait_ge(blank_ready, 1)
                nc.gpsimd.memset(blank[:, D:D + 1], NOWHERE).then_inc(blank_ready, 1)
                pool.wait_ge(m["ld_wq1"], 16)
                nc.gpsimd.tensor_scalar(wq[:, :, :], wq[:, :, :], HD1 ** -0.5, 1.0, ALU.mult, ALU.mult).then_inc(setup_pool, 1)
                pool.wait_ge(blanked, 16)
                last_row = pool.to_reg(NE * CAP - 1)

                def power(ap, done):
                    nc.gpsimd.tensor_tensor(ap, ap, m["halfneg"][:, 0:ap.shape[1]], ALU.pow).then_inc(done, 1)

                def step(t, p, has):
                    if has(1):
                        pool.wait_ge(s_msq, 2 * t - 1)
                        power(meansq[:, 0, :], s_fac)
                    if has(2):
                        pool.wait_ge(g_var, t - 1)
                        power(grstd[:, :], g_rstd)
                    if has(4):
                        pool.wait_ge(g_row, t - 3)
                        pool.wait_ge(g_gate, t - 3)
                        pool.wait_ge(g_slot, t - 3)
                    if has(-3):
                        pool.wait_ge(s_var, t + 4)
                        power(rstd[:, :], s_rstd)
                    if has(4):
                        nc.gpsimd.indirect_dma_start(
                            out=rows, out_offset=bass.IndirectOffsetOnAxis(ap=slot[:, p:p + 1], axis=0),
                            in_=row[:, p, :], in_offset=None, bounds_check=last_row, oob_is_err=False)\
                          .then_inc(m["scattered"][p], 16)
                    if has(1):
                        pool.wait_ge(s_msq, 2 * t)
                        power(meansq[:, 1, :], s_fac)
                    if has(3):
                        q = 1 - p
                        if has(5):
                            pool.wait_ge(m["scattered"][q], 8 * (t - 3 - q))
                        nc.gpsimd.tensor_copy(row[:, q, 0:D], h[:, bass.ds(t - 3, 1), :].squeeze(1))
                        nc.gpsimd.tensor_copy(row[:, q, D:D + 1], c128[:, bass.ds(C_TOK + t - 3, 1)]).then_inc(g_row, 1)

                steps(step, pool)

            @block.tensor
            def _(pe):
                pe.wait_ge(setup_pool, 2)
                pe.wait_ge(setup_dve, 1)
                pe.wait_ge(ld_wg, 16)
                pe.wait_ge(m["ld_wk1"], 16)
                pe.wait_ge(m["ld_wv1"], 16)

                def fill(t, j, par):
                    if j == 0:
                        pe.wait_ge(s_xnT, t + 1)
                    w = (wq, wq, wk, wk, wv, wv)[j]
                    if j < 4:
                        for c in range(4):
                            n = 4 * (j % 2) + c
                            for k in range(2):
                                mm = nc.tensor.matmul(bank[:, BP, c * P:(c + 1) * P], w[:, k, n * P:(n + 1) * P],
                                                      xnT[:, par, k, :], start=(k == 0), stop=(k == 1))
                    else:
                        for k in range(2):
                            mm = nc.tensor.matmul(bank[:, BP, :], xnT[:, par, k, :],
                                                  w[:, k, 512 * (j - 4):512 * (j - 3)], start=(k == 0), stop=(k == 1))
                    mm.then_inc(s_fill, 1)

                def scores(q, p):
                    for c in range(4):
                        n = 4 * q + c
                        for s in range(2):
                            mm = nc.tensor.matmul(bank[:, 2 * q + s, c * P:(c + 1) * P], qT[64 * s:64 * s + 64, p, n, :],
                                                  kT[64 * s:64 * s + 64, p, n, :], start=True, stop=True)
                    mm.then_inc(s_score, 1)

                def turn(src, b, done):
                    for c in range(4):
                        mm = nc.tensor.transpose(bank[:, b, c * P:(c + 1) * P], src[:, c, :], ident)
                    mm.then_inc(done, 1)

                def outputs(q, par):
                    for c in range(4):
                        n = 4 * q + c
                        mm = nc.tensor.matmul(bank[:, BV, c * P:(c + 1) * P], diffT[:, q, c, :],
                                              val[:, par, n * P:(n + 1) * P], start=True, stop=True)
                    mm.then_inc(s_pv, 1)

                def step(t, p, has):
                    o = 1 - p
                    if has(0):
                        pe.wait_ge(s_fa, 3 * t + 2)
                        if has(1):
                            pe.wait_ge(s_exp, 2 * t - 1)
                        scores(0, p)
                    if has(-1):
                        if has(0):
                            pe.wait_ge(s_fd, 3 * t + 3)
                        fill(t + 1, 0, o)
                    if has(1):
                        pe.wait_ge(s_norm, 2 * t - 1)
                        if has(2):
                            pe.wait_ge(s_res, t - 1)
                        turn(normed[:, 0], BX, s_nT_ps)
                    if has(1):
                        pe.wait_ge(s_diff, 2 * t)
                        if has(3):
                            pe.wait_ge(g_lg, t - 2)
                        turn(diff[:, 1], BD, s_dT_ps)
                    if has(-1):
                        pe.wait_ge(s_fa, 3 * t + 4)
                        fill(t + 1, 1, o)
                    if has(1):
                        pe.wait_ge(s_dT, 2 * t)
                        pe.wait_ge(s_fd, 3 * t)
                        pe.wait_ge(s_norm, 2 * t - 1)
                        outputs(1, o)
                    if has(-1):
                        pe.wait_ge(s_fd, 3 * t + 4)
                        fill(t + 1, 2, o)
                    if has(-2):
                        pe.wait_ge(s_xn, t + 3)
                        for k in range(2):
                            mm = nc.tensor.transpose(bank[:, BD, k * P:(k + 1) * P], xn[:, p, k * P:(k + 1) * P], ident)
                        mm.then_inc(s_xnT_ps, 1)
                    if has(3):
                        pe.wait_ge(g_hot, t - 2)
                        if has(4):
                            pe.wait_ge(g_sum, t - 3)
                        nc.tensor.matmul(bank[:, BD, D:D + NE], c128[:, C_TRI:C_TRI + P], hot[:, :], start=True, stop=False)
                        nc.tensor.matmul(bank[:, BD, D:D + NE], ones[:, :], hotsum[:, :], start=False, stop=True)\
                          .then_inc(g_ps, 1)
                    if has(2):
                        pe.wait_ge(g_norm, t - 1)
                        if has(1):
                            pe.wait_ge(s_nT, 2 * t - 1)
                        else:
                            pe.wait_ge(s_res, t - 1)
                        for k in range(2):
                            mm = nc.tensor.transpose(bank[:, BX, k * P:(k + 1) * P], gn[:, k * P:(k + 1) * P], ident)
                        mm.then_inc(g_T_ps, 1)
                    if has(0):
                        pe.wait_ge(s_fd, 3 * t + 2)
                        if has(1):
                            pe.wait_ge(s_exp, 2 * t)
                        scores(1, p)
                    if has(-1):
                        pe.wait_ge(s_fa, 3 * t + 5)
                        fill(t + 1, 3, o)
                    if has(1):
                        pe.wait_ge(s_norm, 2 * t)
                        if has(2):
                            pe.wait_ge(g_T, t - 1)
                        turn(normed[:, 1], BX, s_nT_ps)
                    if has(0):
                        pe.wait_ge(s_diff, 2 * t + 1)
                        if has(-2):
                            pe.wait_ge(s_xnT, t + 3)
                        if has(3):
                            pe.wait_ge(g_pos, t - 2)
                        turn(diff[:, 0], BD, s_dT_ps)
                    if has(-1):
                        pe.wait_ge(s_fd, 3 * t + 5)
                        fill(t + 1, 4, o)
                    if has(0):
                        pe.wait_ge(s_dT, 2 * t + 1)
                        pe.wait_ge(s_fa, 3 * t + 3)
                        if has(1):
                            pe.wait_ge(s_norm, 2 * t)
                        outputs(0, p)
                    if has(-1):
                        pe.wait_ge(s_fa, 3 * t + 6)
                        fill(t + 1, 5, o)
                    if has(1):
                        pe.wait_ge(s_nT, 2 * t)
                        for n in range(H1):
                            mm = nc.tensor.matmul(bank[:, BX, 0:D], normedT[:, n // 4, n % 4, :], wo[:, n, :],
                                                  start=(n == 0), stop=(n == H1 - 1))
                        mm.then_inc(s_wo, 1)
                    if has(2):
                        pe.wait_ge(g_T, t - 1)
                        if not has(0) and has(3):
                            pe.wait_ge(g_pos, t - 2)
                        for k in range(2):
                            mm = nc.tensor.matmul(bank[:, BD, 0:NE], gnT[:, k, :], wg[:, k, :], start=(k == 0), stop=(k == 1))
                        mm.then_inc(g_lg_ps, 1)

                steps(step, pe)

            @block.vector
            def _(dve):
                dve.wait_ge(m["ld_lq"], 64)
                nc.vector.tensor_tensor(lprod[:, :, :], lq[:, 0:4:2, :], lq[:, 1:4:2, :], ALU.mult).then_inc(s_lprod, 1)
                dve.wait_ge(s_lprod, 1)
                nc.vector.tensor_reduce(lsum[:, :], lprod[:, :, :], AX.X, ALU.add).then_inc(s_lsum, 1)
                dve.wait_ge(m["ld_subln"], 16)
                dve.wait_ge(m["ld_wo1"], 16)
                nc.vector.tensor_scalar(wo[:, :, :], wo[:, :, :], m["subln"][:, 0:1], 1.0 - LAMBDA_INIT, ALU.mult, ALU.mult)
                dve.wait_ge(s_lexp, 1)
                nc.vector.tensor_tensor(neglam[:, :], lexp[:, 1:2], lexp[:, 0:1], ALU.subtract).then_inc(s_lam, 1)
                dve.wait_ge(s_lam, 1)
                nc.vector.tensor_scalar(neglam[:, :], neglam[:, :], -LAMBDA_INIT, None, ALU.add).then_inc(setup_dve, 1)
                dve.wait_ge(setup_dve, 1)
                dve.wait_ge(ld_bg, 16)

                def quad(ap):
                    return ap.rearrange("p (c n) -> p c n", c=4)

                def take(j, t, par):
                    dve.wait_ge(s_fill, 6 * t + j + 1)
                    if j < 4:
                        dst = (qT, kT)[j // 2][:, par, 4 * (j % 2):4 * (j % 2) + 4, :]
                        nc.vector.tensor_copy(dst, quad(bank[:, BP, :])).then_inc(s_fd, 1)
                    else:
                        nc.vector.tensor_copy(val[:, par, 512 * (j - 4):512 * (j - 3)], bank[:, BP, :]).then_inc(s_fd, 1)

                def maxima(n, q):
                    dve.wait_ge(s_score, n + 1)
                    nc.vector.tensor_reduce(negmax[:, q, :], bank[:, 2 * q:2 * q + 2, :].rearrange("p s (c k) -> p (s c) k", c=4),
                                            AX.X, ALU.max, negate=True).then_inc(s_max, 1)

                def mean_square(n, q):
                    dve.wait_ge(s_sq, n + 1)
                    nc.vector.scalar_tensor_tensor(out=meansq[:, q, :], in0=ssq[:, q, :], scalar=1.0 / P, in1=epsum[:, q, :],
                                                   op0=ALU.mult, op1=ALU.add).then_inc(s_msq, 1)

                def normalise(n, q):
                    dve.wait_ge(s_fac, n + 1)
                    nc.vector.tensor_tensor(normed[:, q], quad(bank[:, BV, :]),
                                            meansq[:, q, :].unsqueeze(2).to_broadcast([P, 4, P]), ALU.mult).then_inc(s_norm, 1)

                def combine(n, q):
                    dve.wait_ge(s_exp, n + 1)
                    nc.vector.reciprocal(rsec[:, :], psum_[:, q, 4:8]).then_inc(s_rsec, 1)
                    nc.vector.scalar_tensor_tensor(out=epsum[:, q, :], in0=psum_[:, q, 0:4], scalar=EPS,
                                                   in1=psum_[:, q, 0:4], op0=ALU.mult, op1=ALU.mult)
                    dve.wait_ge(s_rsec, n + 1)
                    nc.vector.scalar_tensor_tensor(out=ratio[:, :], in0=psum_[:, q, 0:4], scalar=neglam[:, 0:1],
                                                   in1=rsec[:, :], op0=ALU.mult, op1=ALU.mult).then_inc(s_ratio, 1)
                    dve.wait_ge(s_ratio, n + 1)
                    for c in range(4):
                        mm = nc.vector.scalar_tensor_tensor(out=diff[:, q, c, :], in0=prob[:, q, 4 + c, :],
                                                            scalar=ratio[:, c:c + 1], in1=prob[:, q, c, :],
                                                            op0=ALU.mult, op1=ALU.add)
                    mm.then_inc(s_diff, 1)

                def step(t, p, has):
                    o = 1 - p
                    if has(3):
                        dve.wait_ge(g_lg_ps, t - 2)
                        nc.vector.tensor_tensor(logit[:, :], bank[:, BD, 0:NE], bg[:, :], ALU.add).then_inc(g_lg, 1)
                    if has(2):
                        dve.wait_ge(s_res, t - 1)
                    if has(1):
                        mean_square(2 * t - 2, 0)
                    if has(2):
                        nc.vector.bn_stats(gstats[:, :], h[:, bass.ds(t - 2, 1), :].squeeze(1)).then_inc(g_stat, 1)
                        dve.wait_ge(g_stat, t - 1)
                    if has(0):
                        maxima(2 * t, 0)
                    if has(2):
                        nc.vector.bn_aggr(gmeanvar[:, :], gstats[:, :]).then_inc(g_mean, 1)
                        dve.wait_ge(g_mean, t - 1)
                        nc.vector.tensor_scalar(grstd[:, :], gmeanvar[:, 1:2], EPS, None, ALU.add).then_inc(g_var, 1)
                    if has(1):
                        normalise(2 * t - 2, 0)
                        combine(2 * t - 1, 1)
                    if has(1):
                        dve.wait_ge(s_nT_ps, 2 * t - 1)
                        nc.vector.tensor_copy(normedT[:, 0], quad(bank[:, BX, :])).then_inc(s_nT, 1)
                    if has(-3):
                        nc.vector.bn_stats(stats[:, :], h[:, bass.ds(t + 3, 1), :].squeeze(1)).then_inc(s_stat, 1)
                    if has(2):
                        dve.wait_ge(g_rstd, t - 1)
                        nc.vector.tensor_scalar(gn[:, :], h[:, bass.ds(t - 2, 1), :].squeeze(1), gmeanvar[:, 0:1],
                                                grstd[:, 0:1], ALU.subtract, ALU.mult).then_inc(g_norm, 1)
                    if has(-3):
                        dve.wait_ge(s_stat, t + 4)
                    if has(1):
                        dve.wait_ge(s_dT_ps, 2 * t)
                        nc.vector.tensor_copy(diffT[:, 1], quad(bank[:, BD, :])).then_inc(s_dT, 1)
                    if has(-3):
                        nc.vector.bn_aggr(meanvar[:, :], stats[:, :]).then_inc(s_mean, 1)
                        dve.wait_ge(s_mean, t + 4)
                        nc.vector.tensor_scalar(rstd[:, :], meanvar[:, 1:2], EPS, None, ALU.add).then_inc(s_var, 1)
                    if has(3):
                        dve.wait_ge(g_lg, t - 2)
                        nc.vector.tensor_reduce(glmax[:, :], logit[:, :], AX.X, ALU.max).then_inc(g_max, 1)
                        dve.wait_ge(g_max, t - 2)
                        nc.vector.tensor_scalar(gnegmax[:, :], glmax[:, :], -1.0, None, ALU.mult).then_inc(g_neg, 1)
                        nc.vector.tensor_scalar(top[:, :], logit[:, :], glmax[:, 0:1], None, ALU.is_equal).then_inc(g_top, 1)
                        dve.wait_ge(g_top, t - 2)
                        nc.vector.scalar_tensor_tensor(out=cand[:, :], in0=top[:, :], scalar=-64.0,
                                                       in1=c128[:, C_EXP:C_EXP + NE], op0=ALU.mult, op1=ALU.add).then_inc(g_cand, 1)
                        dve.wait_ge(g_cand, t - 2)
                        nc.vector.tensor_reduce(first[:, :], cand[:, :], AX.X, ALU.min).then_inc(g_first, 1)
                        dve.wait_ge(g_first, t - 2)
                        nc.vector.tensor_scalar(hot[:, :], cand[:, :], first[:, 0:1], None, ALU.is_equal).then_inc(g_hot, 1)
                    if has(-1):
                        take(1, t + 1, o)
                    if has(2):
                        dve.wait_ge(g_T_ps, t - 1)
                        nc.vector.tensor_copy(gnT[:, :, :], bank[:, BX, 0:D].rearrange("p (k n) -> p k n", k=2)).then_inc(g_T, 1)
                    if has(1):
                        mean_square(2 * t - 1, 1)
                    if has(-2):
                        dve.wait_ge(s_xnT_ps, t + 3)
                        nc.vector.tensor_copy(xnT[:, p], bank[:, BD, 0:D].rearrange("p (k n) -> p k n", k=2)).then_inc(s_xnT, 1)
                    if has(0):
                        maxima(2 * t + 1, 1)
                    if has(1):
                        normalise(2 * t - 1, 1)
                    if has(0):
                        combine(2 * t, 0)
                    if has(3):
                        dve.wait_ge(g_ps, t - 2)
                        nc.vector.scalar_tensor_tensor(out=posjunk[:, :], in0=bank[:, BD, D:D + NE], scalar=1.0,
                                                       in1=hot[:, :], op0=ALU.mult, op1=ALU.mult,
                                                       accum_out=pos[:, :]).then_inc(g_pos, 1)
                        nc.vector.tensor_tensor(hotsum[:, :], hotsum[:, :], hot[:, :], ALU.add).then_inc(g_sum, 1)
                        dve.wait_ge(g_pos, t - 2)
                        nc.vector.tensor_scalar(over[:, :], pos[:, :], float(CAP), NOWHERE, ALU.is_ge, ALU.mult).then_inc(g_over, 1)
                        nc.vector.scalar_tensor_tensor(out=slotf[:, :], in0=first[:, :], scalar=float(CAP), in1=pos[:, :],
                                                       op0=ALU.mult, op1=ALU.add).then_inc(g_slotf, 1)
                        dve.wait_ge(g_slotf, t - 2)
                        dve.wait_ge(g_over, t - 2)
                        if has(5):
                            dve.wait_ge(m["scattered"][o], 8 * (t - 3 - o))
                        nc.vector.scalar_tensor_tensor(out=slot[:, o:o + 1], in0=slotf[:, :], scalar=64.0 * CAP,
                                                       in1=over[:, :], op0=ALU.add, op1=ALU.add).then_inc(g_slot, 1)
                    if has(-1):
                        take(3, t + 1, o)
                    if has(-3):
                        dve.wait_ge(s_rstd, t + 4)
                        nc.vector.tensor_scalar(xn[:, o], h[:, bass.ds(t + 3, 1), :].squeeze(1), meanvar[:, 0:1],
                                                rstd[:, 0:1], ALU.subtract, ALU.mult).then_inc(s_xn, 1)
                    if has(1):
                        dve.wait_ge(s_nT_ps, 2 * t)
                        nc.vector.tensor_copy(normedT[:, 1], quad(bank[:, BX, :])).then_inc(s_nT, 1)
                    if has(0):
                        dve.wait_ge(s_dT_ps, 2 * t + 1)
                        nc.vector.tensor_copy(diffT[:, 0], quad(bank[:, BD, :])).then_inc(s_dT, 1)
                    if has(3):
                        dve.wait_ge(g_exp, t - 2)
                        nc.vector.reciprocal(row[:, o, D + 1:D + 2], gsum[:, :]).then_inc(g_gate, 1)
                    if has(-1):
                        take(5, t + 1, o)
                    if has(1):
                        dve.wait_ge(s_wo, t)
                        ht = h[:, bass.ds(t - 1, 1), :].squeeze(1)
                        nc.vector.tensor_tensor(ht, ht, bank[:, BX, 0:D], ALU.add).then_inc(s_res, 1)

                steps(step, dve)

            @block.scalar
            def _(act):
                nc.scalar.preload_act_table(ACT.Exp)
                act.wait_ge(s_lsum, 1)
                nc.scalar.activation(lexp[:, :], lsum[:, :], ACT.Exp).then_inc(s_lexp, 1)

                def take(j, t, par):
                    act.wait_ge(s_fill, 6 * t + j + 1)
                    if j < 4:
                        dst = (qT, kT)[j // 2][:, par, 4 * (j % 2):4 * (j % 2) + 4, :]
                        nc.scalar.copy(dst, bank[:, BP, :].rearrange("p (c n) -> p c n", c=4)).then_inc(s_fa, 1)
                    else:
                        nc.scalar.copy(val[:, par, 512 * (j - 4):512 * (j - 3)], bank[:, BP, :]).then_inc(s_fa, 1)

                def softmax(n, q):
                    act.wait_ge(s_max, n + 1)
                    for c in range(8):
                        at = (c % 4) * P
                        mm = nc.scalar.activation(prob[:, q, c, :], bank[:, 2 * q + c // 4, at:at + P], ACT.Exp,
                                                  bias=negmax[:, q, c:c + 1], accum_out=psum_[:, q, c:c + 1])
                    mm.then_inc(s_exp, 1)

                def squares(n, q):
                    act.wait_ge(s_pv, n + 1)
                    for c in range(4):
                        mm = nc.scalar.activation(junk[:, q, c, :], bank[:, BV, c * P:(c + 1) * P], ACT.Square,
                                                  accum_out=ssq[:, q, c:c + 1])
                    mm.then_inc(s_sq, 1)

                def step(t, p, has):
                    o = 1 - p
                    if has(-1):
                        take(0, t + 1, o)
                    if has(0):
                        softmax(2 * t, 0)
                    if has(-1):
                        take(2, t + 1, o)
                    if has(1):
                        squares(2 * t - 1, 1)
                    if has(0):
                        softmax(2 * t + 1, 1)
                    if has(3):
                        act.wait_ge(g_neg, t - 2)
                        nc.scalar.activation(gexp[:, :], logit[:, :], ACT.Exp, bias=gnegmax[:, 0:1],
                                             accum_out=gsum[:, :]).then_inc(g_exp, 1)
                    if has(-1):
                        take(4, t + 1, o)
                    if has(0):
                        squares(2 * t, 0)

                steps(step, act)


def expert_phase(nc, a, m, rows, out):
    bank, c128 = m["bank"], m["c128"]
    ident = c128[:, C_ID:C_ID + P]
    NC = CAP // P
    NH = HID // P
    with ExitStack() as ctx:
        def sb(name, shape, dt=F32):
            return ctx.enter_context(nc.sbuf_tensor(name, shape, dt))

        def sem(name):
            return ctx.enter_context(nc.semaphore(name))

        w1 = sb("w1", [P, 2, 2, HID])
        w2 = sb("w2", [P, 2, NH, D])
        b1 = sb("b1", [P, NE, NH])
        b1raw = sb("b1raw", [NE, HID])
        b2 = sb("b2", [P, 2, D])
        x = sb("x_rows", [P, 2, NC, ROW])
        gate = sb("gate", [P, 2, NC])
        token = sb("token", [P, 2, NC], U32)
        stats = sb("e_stats", [P, NC, 6])
        meanvar = sb("e_meanvar", [P, NC, 2])
        rstd = sb("e_rstd", [P, NC])
        xn = sb("e_xn", [P, NC, D])
        xT = sb("e_xT", [P, 2, 2, CAP])
        hT = sb("e_hT", [P, NH, CAP])
        yb = sb("e_yb", [P, 2, D])
        yg = sb("e_yg", [P, NC, D])
        y = sb("e_y", [P, NC, D])

        ld_w1, ld_w2, ld_b2, ld_x = ([sem(f"e_ld_{n}{i}") for i in range(2)] for n in ("w1_", "w2_", "b2_", "x_"))
        ld_b1, s_b1_ps, s_b1 = sem("e_ld_b1"), sem("e_b1_ps"), sem("e_b1")
        s_stat, s_tok, s_mean, s_var, s_rstd, s_xn, s_xT_ps, s_xT = \
            sem("e_stat"), sem("e_tok"), sem("e_mean"), sem("e_var"), sem("e_rstd"), sem("e_norm"), sem("e_xT_ps"), sem("e_xTs")
        s_h_ps, s_h, s_y_ps, s_yb, s_yg, s_y = \
            sem("e_h_ps"), sem("e_h"), sem("e_y_ps"), sem("e_ybs"), sem("e_ygs"), sem("e_ys")
        sent = [sem(f"e_sent{c}") for c in range(NC)]

        def steps(step, engine):
            def peeled(e):
                step(e, e % 2, lambda lag: 0 <= e - lag < NE)

            peeled(-1)
            peeled(0)
            with engine.Fori(0, NE // 2 - 1) as i:
                for p in (1, 0):
                    step(2 * i + (2 - p), p, lambda lag: True)
            peeled(NE - 1)

        with nc.Block() as block:
            @block.sync
            def _(sp):
                sp.dma_start(b1raw[:, :], a["L1_ffn_b1"]).then_inc(ld_b1, 16)
                sp.wait_ge(m["scattered"][0], 16 * NT // 2)
                sp.wait_ge(m["scattered"][1], 16 * NT // 2)

                def step(e, p, has):
                    q = 1 - p
                    if has(-1):
                        if has(1):
                            sp.wait_ge(s_y, NC * e)
                        sp.dma_start(x[:, q], rows[bass.ds(CAP * (e + 1), CAP), :].rearrange("(c p) d -> p c d", p=P))\
                          .then_inc(ld_x[q], 16)
                        if has(1):
                            sp.wait_ge(s_y_ps, NC * e)
                        sp.dma_start(w1[:, q], a["L1_ffn_W1"][bass.ds(e + 1, 1)].squeeze(0).rearrange("(k p) n -> p k n", p=P))\
                          .then_inc(ld_w1[q], 16)
                        sp.dma_start(w2[:, q], a["L1_ffn_W2"][bass.ds(e + 1, 1)].squeeze(0).rearrange("(k p) n -> p k n", p=P))\
                          .then_inc(ld_w2[q], 16)
                        sp.dma_start(b2[:, q, :], a["L1_ffn_b2"][bass.ds(e + 1, 1), :].to_broadcast([P, D]))\
                          .then_inc(ld_b2[q], 16)

                steps(step, sp)
                for c in range(NC):
                    sp.wait_ge(sent[c], 16 * NE)

            @block.gpsimd
            def _(pool):
                last_token = pool.to_reg(NT * P - 1)
                pool.wait_ge(m["prefilled"], 16 * NT)

                def send(c, p):
                    nc.gpsimd.indirect_dma_start(
                        out=out, out_offset=bass.IndirectOffsetOnAxis(ap=token[:, p, c:c + 1], axis=0),
                        in_=y[:, c, :], in_offset=None, bounds_check=last_token, oob_is_err=False).then_inc(sent[c], 16)

                def step(e, p, has):
                    if has(-1):
                        pool.wait_ge(s_var, e + 2)
                        nc.gpsimd.tensor_tensor(rstd[:, :], rstd[:, :], m["halfneg"][:, 0:NC], ALU.pow).then_inc(s_rstd, 1)
                    if has(0):
                        for c in range(NC):
                            pool.wait_ge(s_yg, NC * e + c + 1)
                            if c == 1:
                                pool.wait_ge(s_tok, e + 1)
                            if has(1):
                                pool.wait_ge(sent[c], 16 * e)
                            if c or has(1):
                                pool.wait_ge(s_y, NC * e + c)
                            nc.gpsimd.tensor_tensor(y[:, c, :], yg[:, c, :], x[:, p, c, 0:D], ALU.add).then_inc(s_y, 1)
                            if c:
                                send(c - 1, p)
                            elif has(1):
                                send(NC - 1, 1 - p)

                steps(step, pool)
                pool.wait_ge(s_y, NC * NE)
                send(NC - 1, (NE - 1) % 2)

            @block.tensor
            def _(pe):
                pe.wait_ge(ld_b1, 16)
                for n in range(NH):
                    mm = nc.tensor.transpose(bank[:, 7, n * NE:(n + 1) * NE], b1raw[:, n * P:(n + 1) * P],
                                             c128[0:NE, C_ID:C_ID + NE])
                mm.then_inc(s_b1_ps, 1)

                def step(e, p, has):
                    q = 1 - p
                    if has(0):
                        pe.wait_ge(s_xT, 2 * e + 2)
                        pe.wait_ge(ld_w1[p], 8 * (e - p) + 16)
                        for n in range(NH):
                            if n >= 2 or has(1):
                                pe.wait_ge(s_h, NH * e + n - 1)
                            for k in range(2):
                                mm = nc.tensor.matmul(bank[:, n % 2, :], w1[:, p, k, n * P:(n + 1) * P], xT[:, p, k, :],
                                                      start=(k == 0), stop=(k == 1))
                            mm.then_inc(s_h_ps, 1)
                    if has(-1):
                        pe.wait_ge(s_xn, e + 2)
                        for k in range(2):
                            if has(0):
                                pe.wait_ge(s_xT, 2 * e + 1 + k)
                            for c in range(NC):
                                mm = nc.tensor.transpose(bank[:, 4 + k, c * P:(c + 1) * P], xn[:, c, k * P:(k + 1) * P], ident)
                            mm.then_inc(s_xT_ps, 1)
                    if has(0):
                        pe.wait_ge(ld_w2[p], 8 * (e - p) + 16)
                        pe.wait_ge(s_h, NH * e + NH)
                        for c in range(NC):
                            if c >= 2 or has(1):
                                pe.wait_ge(s_yb, NC * e + c - 1)
                            for n in range(NH):
                                mm = nc.tensor.matmul(bank[:, 2 + c % 2, 0:D], hT[:, n, c * P:(c + 1) * P], w2[:, p, n, :],
                                                      start=(n == 0), stop=(n == NH - 1))
                            mm.then_inc(s_y_ps, 1)

                steps(step, pe)

            @block.vector
            def _(dve):
                dve.wait_ge(s_b1_ps, 1)
                nc.vector.tensor_copy(b1[:, :, :], bank[:, 7, 0:NH * NE].rearrange("p (n e) -> p e n", e=NE)).then_inc(s_b1, 1)

                def step(e, p, has):
                    q = 1 - p
                    if has(-1):
                        dve.wait_ge(ld_x[q], 8 * (e + 1 - q) + 16)
                        for c in range(NC):
                            mm = nc.vector.bn_stats(stats[:, c, :], x[:, q, c, 0:D])
                        mm.then_inc(s_stat, 1)
                        dve.wait_ge(s_stat, e + 2)
                        nc.vector.tensor_copy(gate[:, q, :], x[:, q, :, D + 1])
                        for c in range(NC):
                            mm = nc.vector.bn_aggr(meanvar[:, c, :], stats[:, c, :])
                        mm.then_inc(s_mean, 1)
                        dve.wait_ge(s_mean, e + 2)
                        nc.vector.tensor_scalar(rstd[:, :], meanvar[:, :, 1], EPS, None, ALU.add).then_inc(s_var, 1)
                        dve.wait_ge(s_rstd, e + 2)
                        for c in range(NC):
                            mm = nc.vector.tensor_scalar(xn[:, c, :], x[:, q, c, 0:D], meanvar[:, c, 0:1], rstd[:, c:c + 1],
                                                         ALU.subtract, ALU.mult)
                        mm.then_inc(s_xn, 1)
                        for k in range(2):
                            dve.wait_ge(s_xT_ps, 2 * e + 3 + k)
                            nc.vector.tensor_copy(xT[:, q, k, :], bank[:, 4 + k, :]).then_inc(s_xT, 1)
                    if has(0):
                        dve.wait_ge(ld_b2[p], 8 * (e - p) + 16)
                        for c in range(NC):
                            dve.wait_ge(s_y_ps, NC * e + c + 1)
                            nc.vector.tensor_tensor(yb[:, c % 2, :], bank[:, 2 + c % 2, 0:D], b2[:, p, :], ALU.add)\
                              .then_inc(s_yb, 1)
                            if has(1):
                                dve.wait_ge(s_y, NC * (e - 1) + c + 1)
                            dve.wait_ge(s_yb, NC * e + c + 1)
                            nc.vector.tensor_scalar(yg[:, c, :], yb[:, c % 2, :], gate[:, p, c:c + 1], None, ALU.mult)\
                              .then_inc(s_yg, 1)
                    if has(-1):
                        if has(1):
                            dve.wait_ge(sent[NC - 1], 16 * e)
                        nc.vector.tensor_copy(token[:, q, :], x[:, q, :, D]).then_inc(s_tok, 1)

                steps(step, dve)

            @block.scalar
            def _(act):
                nc.scalar.preload_act_table(ACT.Relu)
                act.wait_ge(s_b1, 1)

                def step(e, p, has):
                    if has(0):
                        for n in range(NH):
                            act.wait_ge(s_h_ps, NH * e + n + 1)
                            nc.scalar.activation(hT[:, n, :], bank[:, n % 2, :], ACT.Relu,
                                                 bias=b1[:, bass.ds(e, 1), n:n + 1].squeeze(1)).then_inc(s_h, 1)

                steps(step, act)


def shape_constants():
    import numpy as np

    c = np.zeros((P, C_COLS), np.float32)
    r = np.arange(P)
    c[:, C_ID:C_ID + P] = np.eye(P)
    c[:, C_MASK:C_MASK + P] = np.where(r[None, :] <= r[:, None], 0.0, MASKED)
    c[:, C_TRI:C_TRI + P] = r[:, None] < r[None, :]
    c[:, C_VOC:C_VOC + P] = r[None, :] % V
    c[:, C_EXP:C_EXP + NE] = np.arange(NE)[None, :]
    c[:, C_TOK:C_TOK + NT] = r[:, None] + P * np.arange(NT)[None, :]
    c[:, C_PART] = r
    c2 = np.zeros((V, C2_COLS), np.float32)
    for t in range(NFRAME):
        for n in range(V):
            s = V * t + n - V // 2
            s = -s if s < 0 else (2 * (P - 1) - s if s >= P else s)
            c2[n, C2_FRAME + P * t + s] = 1.0
    n, f = np.arange(V)[:, None], np.arange(NFREQ)[None, :]
    c2[:, C2_DFT:C2_DFT + NFREQ] = np.cos(2 * np.pi * n * f / V)
    c2[:, C2_DFT + NFREQ:C2_DFT + NREIM] = np.sin(2 * np.pi * n * f / V)
    wi = np.zeros((NFRAME + 1, P), np.float32)
    at = np.clip((np.arange(P) + 0.5) * (NFRAME / P) - 0.5, 0.0, NFRAME - 1.0)
    lo = np.floor(at).astype(int)
    hi = np.minimum(lo + 1, NFRAME - 1)
    w = (at - lo).astype(np.float32)
    np.add.at(wi, (lo, np.arange(P)), 1.0 - w)
    np.add.at(wi, (hi, np.arange(P)), w)
    wi[NFRAME] = 1.0
    return {"c_128": c, "c_64": c2, "c_interp": wi}


_INS = ['x', 'L0_tok_emb_table', 'L0_tok_proj_w', 'L0_tok_proj_b', 'L0_tok_window', 'L0_attn_w_attn',
        'L0_attn_w_proj', 'L0_ffn_ternary_weight', 'L0_ffn_bias', 'L0_ffn_act_scale', 'L1_attn_Wq', 'L1_attn_Wk',
        'L1_attn_Wv', 'L1_attn_Wo', 'L1_attn_lq1', 'L1_attn_lk1', 'L1_attn_lq2', 'L1_attn_lk2', 'L1_attn_subln_w',
        'L1_ffn_Wg', 'L1_ffn_bg', 'L1_ffn_W1', 'L1_ffn_b1', 'L1_ffn_W2', 'L1_ffn_b2']


def kernel(**inputs):
    import numpy as _np
    import concourse.bacc as _bacc
    from concourse.bass_utils import run_bass_kernel_spmd as _run

    nc = _bacc.Bacc("TRN2", target_bir_lowering=False, num_devices=1)
    arrays, args = {}, {}
    held = {name: _np.ascontiguousarray(inputs[name]) for name in _INS}
    held["L0_ffn_act_scale"] = held["L0_ffn_act_scale"].reshape(1)
    held.update(shape_constants())
    for name, a in held.items():
        arrays[f"in_{name}"] = a
        args[name] = nc.dram_tensor(f"in_{name}", a.shape, mybir.dt.from_np(a.dtype), kind="ExternalInput").ap()
    out = nc.dram_tensor("out_0", (NT * P, D), F32, kind="ExternalOutput").ap()
    rows = nc.dram_tensor("dispatched_rows", (NE * CAP, ROW), F32, kind="Internal").ap()
    tower_kernel(nc, args, rows, out)
    r = _run(nc, [arrays], core_ids=[0])
    return r.results[0]["out_0"].reshape(NT, P, D)
```

```python
from contextlib import ExitStack

import concourse.bass as bass
from concourse import mybir

F32 = mybir.dt.float32
F32R = mybir.dt.float32r
BF16 = mybir.dt.bfloat16
I32 = mybir.dt.int32
U32 = mybir.dt.uint32
ALU = mybir.AluOpType
ACT = mybir.ActivationFunctionType
AX = mybir.AxisListType

P = 128
NT = 64
D = 256
V = 64
NEMB = 179
NSTFT = D - NEMB
NFRAME = 3
NFREQ = 33
NREIM = 2 * NFREQ
NJ = 17
H0, HD0 = 16, 16
H1, HD1 = 8, 64
NE, HID, CAP = 16, 1024, 512
LAMBDA_INIT = 0.8 - 0.6 * 2.718281828459045 ** (-0.3 * 12)
EPS = 1e-5
ROUND = 12582912.0
MASKED = -1e30
NOWHERE = 65536.0
ROW = D + 2

C_ID, C_MASK, C_TRI, C_VOC, C_EXP, C_TOK, C_VID, C_HALF, C_LOW = 0, 128, 256, 384, 512, 528, 592, 593, 594
C_COLS = 595
C2_FRAME, C2_DFT, C2_COLS = 0, NFRAME * P, NFRAME * P + NREIM


def tower_kernel(nc, a, rows, out):
    with ExitStack() as ctx:
        def psum(name, shape, dt):
            return ctx.enter_context(nc.psum_tensor(name, shape, dt))

        m = {}
        m["bank"] = psum("bank", [P, 8, 512], F32)
        for name, shape, dt in (
            ("h", [P, NT, D], F32), ("c128", [P, C_COLS], F32), ("identb", [P, P], BF16), ("maskb", [P, P], BF16),
            ("halfneg", [P, 8], F32),
        ):
            m[name] = ctx.enter_context(nc.sbuf_tensor(name, shape, dt))
        for name in ("wq1", "wk1", "wv1", "wo1", "subln", "lq"):
            m["ld_" + name] = ctx.enter_context(nc.semaphore("ld_" + name))
        m["scattered"] = [ctx.enter_context(nc.semaphore(f"scattered_{i}")) for i in range(2)]
        m["prefilled"] = ctx.enter_context(nc.semaphore("prefilled"))
        with ExitStack() as weights:
            for name, shape in (("wq1", [P, 2, 1024]), ("wk1", [P, 2, 1024]), ("wv1", [P, 2, 1024]),
                                ("wo1", [P, 8, D]), ("subln", [P, 1]), ("lq", [P, 4, HD1])):
                m[name] = weights.enter_context(nc.sbuf_tensor(name, shape, F32))
            token_phase(nc, a, m)
            for name, shape in (("wv_high", [P, 2, 1024]), ("wv_low", [P, 2, 1024]),
                                ("wo_high", [P, 8, D]), ("wo_low", [P, 8, D])):
                m[name] = weights.enter_context(nc.sbuf_tensor(name, shape, F32R))
            layer0_phase(nc, a, m)
            layer1_phase(nc, a, m, rows, out)
        expert_phase(nc, a, m, rows, out)


def token_phase(nc, a, m):
    bank, h, c128 = m["bank"], m["h"], m["c128"]
    with ExitStack() as ctx:
        def sb(name, shape, dt=F32):
            return ctx.enter_context(nc.sbuf_tensor(name, shape, dt))

        m["used_sems"] = used = []

        def sem(name):
            used.append(ctx.enter_context(nc.semaphore(name)))
            return used[-1]

        c64 = sb("c64", [V, C2_COLS])
        interp = sb("interp", [NFRAME + 1, P])
        ids_row = sb("ids_row", [P, NT * P], I32)
        ids_i = sb("ids_i", [NT, P], I32)
        ids_f = sb("ids_f", [NT, P])
        ids_col = sb("ids_col", [P, NT])
        window = sb("window", [V, 1])
        emb_raw = sb("emb_raw", [P, NEMB + 1])
        emb_high = sb("emb_high", [P, NEMB + 1], F32R)
        emb = sb("emb", [P, NEMB + 1], F32R)
        projraw = sb("projraw", [NSTFT, NFREQ * V])
        projw = sb("projw", [P, NJ, NSTFT])
        wdft = sb("wdft", [V, NREIM])
        dft_high = sb("dft_high", [P, NFRAME * NREIM], F32R)
        dft_low = sb("dft_low", [P, NFRAME * NREIM], F32R)
        hot = sb("hot", [P, 4, 2, P], F32R)
        square = sb("square", [P, 2, 2, NFRAME, NREIM])
        mag = sb("mag", [P, NJ, NFRAME, NT])
        spec = sb("spec", [NT, NFRAME * NSTFT])
        specrow = sb("specrow", [NFRAME + 1, NT, NSTFT])
        mag_dummy = sb("mag_dummy", [P, 3])
        hot_t = sb("hot_t", [P, 4, 2, P], F32R)

        ld_c128, ld_c64, ld_ids, ld_window = sem("t_ld_c128"), sem("t_ld_c64"), sem("t_ld_ids"), sem("t_ld_window")
        ld_row, ld_emb, ld_proj = sem("t_ld_row"), sem("t_ld_emb"), sem("t_ld_proj")
        ld_interp, ld_bias, ld_spec = sem("t_ld_interp"), sem("t_ld_bias"), sem("t_ld_spec")
        ids_ready, wdft_ready, setup_pe, dft_ready = sem("t_ids_ready"), sem("t_wdft"), sem("t_setup_pe"), sem("t_dft")
        projw_ready, mag_clear, idcol_ready = sem("t_projw"), sem("t_magclear"), sem("t_idcol")
        hot_ready, dft_done, squared, summed = sem("t_hot"), sem("t_dftdone"), sem("t_squared"), sem("t_summed")
        rooted, spec_done, spec_ready = sem("t_rooted"), sem("t_specdone"), sem("t_spec")
        dft_split, emb_split, emb_ready = sem("t_dftsplit"), sem("t_embsplit"), sem("t_emb")
        hot_t_ready, tok_done, tok_stored = sem("t_hott"), sem("t_tokdone"), sem("t_tokstored")

        with nc.Block() as block:
            @block.sync
            def _(sp):
                sp.dma_start(c128[:, :], a["c_128"]).then_inc(ld_c128, 16)
                sp.dma_start(c64[:, :], a["c_64"]).then_inc(ld_c64, 16)
                sp.dma_start(window[:, :], a["L0_tok_window"].unsqueeze(1)).then_inc(ld_window, 16)
                sp.dma_start(ids_i[:, :], a["x"]).then_inc(ld_ids, 16)
                sp.dma_start(projraw[:, :], a["L0_tok_proj_w"]).then_inc(ld_proj, 16)
                sp.dma_start(ids_row[:, :], a["x"].rearrange("b l -> (b l)").unsqueeze(0).to_broadcast([P, NT * P]))\
                  .then_inc(ld_row, 16)
                sp.wait_ge(mag_clear, 2)
                for half in range(2):
                    sp.dma_start(emb_raw[half * V:(half + 1) * V, 0:NEMB], a["L0_tok_emb_table"]).then_inc(ld_emb, 16)
                sp.dma_start(interp[:, :], a["c_interp"]).then_inc(ld_interp, 16)
                sp.dma_start(specrow[NFRAME:NFRAME + 1, :, :],
                             a["L0_tok_proj_b"].unsqueeze(0).unsqueeze(0).to_broadcast([1, NT, NSTFT]))\
                  .then_inc(ld_bias, 16)
                sp.wait_ge(spec_ready, 1)
                for t in range(NFRAME):
                    sp.dma_start(specrow[t:t + 1, :, :], spec[:, t * NSTFT:(t + 1) * NSTFT]).then_inc(ld_spec, 16)

            @block.gpsimd
            def _(pool):
                nc.gpsimd.memset(mag[:, :, :, :], 0.0).then_inc(mag_clear, 1)
                nc.gpsimd.memset(emb_raw[:, NEMB:NEMB + 1], 0.0)
                nc.gpsimd.memset(mag_dummy[:, 0:1], 0.0).then_inc(squared, 2)
                nc.gpsimd.memset(mag_dummy[:, 1:2], 0.0).then_inc(summed, 2)
                nc.gpsimd.memset(mag_dummy[:, 2:3], 0.0).then_inc(tok_stored, 4)
                nc.gpsimd.memset(m["halfneg"][:, :], -0.5).then_inc(mag_clear, 1)

            @block.tensor
            def _(pe):
                pe.wait_ge(wdft_ready, 1)
                for t in range(NFRAME):
                    mm = nc.tensor.matmul(bank[:, 0, t * NREIM:(t + 1) * NREIM], c64[:, C2_FRAME + P * t:C2_FRAME + P * (t + 1)],
                                          wdft[:, :], start=True, stop=True)
                mm.then_inc(setup_pe, 1)
                pe.wait_ge(ids_ready, 1)
                nc.tensor.transpose(bank[:, 1, 0:NT], ids_f[:, :], c128[0:NT, C_ID:C_ID + NT]).then_inc(setup_pe, 1)
                pe.wait_ge(ld_proj, 16)
                for j in range(NJ):
                    w = P if j < NJ - 1 else V
                    at = (j % 6) * NSTFT
                    mm = nc.tensor.transpose(bank[0:w, 2 + j // 6, at:at + NSTFT], projraw[:, P * j:P * j + w],
                                             c128[0:NSTFT, C_ID:C_ID + NSTFT])
                mm.then_inc(setup_pe, 1)
                pe.wait_ge(dft_ready, 1)
                with pe.Fori(0, NT // 8) as i:
                    for p in range(4):
                        n = 4 * i + p
                        pe.wait_ge(hot_ready, n + 1)
                        pe.wait_ge(squared, n + 1)
                        for b in range(2):
                            o = bank[:, 5 + p % 2, b * NFRAME * NREIM:(b + 1) * NFRAME * NREIM]
                            nc.tensor.matmul(o, hot[:, p, b, :], dft_low[:, :], start=True, stop=False)
                            mm = nc.tensor.matmul(o, hot[:, p, b, :], dft_high[:, :], start=False, stop=True)
                        mm.then_inc(dft_done, 1)
                pe.wait_ge(rooted, 1)
                pe.wait_ge(projw_ready, 1)
                for t in range(NFRAME):
                    for j in range(NJ):
                        w = P if j < NJ - 1 else V
                        mm = nc.tensor.matmul(bank[0:NT, 7, t * NSTFT:(t + 1) * NSTFT], mag[0:w, j, t, :],
                                              projw[0:w, j, :], start=(j == 0), stop=(j == NJ - 1))
                mm.then_inc(spec_done, 1)
                pe.wait_ge(emb_ready, 1)
                pe.wait_ge(ld_interp, 16)
                pe.wait_ge(ld_bias, 16)
                pe.wait_ge(ld_spec, 16 * NFRAME)
                with pe.Fori(0, NT // 8) as i:
                    for p in range(4):
                        n = 4 * i + p
                        pe.wait_ge(hot_t_ready, n + 1)
                        pe.wait_ge(tok_stored, n + 1)
                        for b in range(2):
                            nc.tensor.matmul(bank[:, p, b * D:b * D + NEMB + 1], hot_t[:, p, b, :], emb[:, :],
                                             start=True, stop=True)
                        nc.tensor.matmul(bank[:, p, :].rearrange("p (b d) -> p b d", b=2)[:, :, NEMB:D], interp[:, :],
                                         specrow[:, bass.ds(2 * n, 2), :], start=True, stop=True).then_inc(tok_done, 1)

            @block.vector
            def _(dve):
                dve.wait_ge(ld_ids, 16)
                nc.vector.tensor_copy(ids_f[:, :], ids_i[:, :]).then_inc(ids_ready, 1)
                dve.wait_ge(ld_c128, 16)
                nc.vector.tensor_copy(m["identb"][:, :], c128[:, C_ID:C_ID + P])
                nc.vector.tensor_copy(m["maskb"][:, :], c128[:, C_MASK:C_MASK + P])
                dve.wait_ge(ld_c64, 16)
                dve.wait_ge(ld_window, 16)
                nc.vector.tensor_scalar(wdft[:, :], c64[:, C2_DFT:C2_DFT + NREIM], window[:, 0:1], None, ALU.mult)\
                  .then_inc(wdft_ready, 1)
                dve.wait_ge(setup_pe, 1)
                nc.vector.tensor_copy(dft_high[:, :], bank[:, 0, 0:NFRAME * NREIM]).then_inc(dft_split, 1)
                dve.wait_ge(dft_split, 1)
                nc.vector.tensor_tensor(dft_low[:, :], bank[:, 0, 0:NFRAME * NREIM], dft_high[:, :].bitcast(F32),
                                        ALU.subtract).then_inc(dft_ready, 1)
                dve.wait_ge(setup_pe, 2)
                nc.vector.tensor_copy(ids_col[:, :], bank[:, 1, 0:NT]).then_inc(idcol_ready, 1)
                dve.wait_ge(setup_pe, 3)
                nc.vector.tensor_copy(projw[:, 0:6, :], bank[:, 2, 0:6 * NSTFT].rearrange("p (j o) -> p j o", j=6))
                nc.vector.tensor_copy(projw[:, 6:12, :], bank[:, 3, 0:6 * NSTFT].rearrange("p (j o) -> p j o", j=6))
                nc.vector.tensor_copy(projw[:, 12:16, :], bank[:, 4, 0:4 * NSTFT].rearrange("p (j o) -> p j o", j=4))
                nc.vector.tensor_copy(projw[0:V, 16, :], bank[0:V, 4, 4 * NSTFT:5 * NSTFT]).then_inc(projw_ready, 1)
                dve.wait_ge(mag_clear, 2)

                def one_hots(n, p):
                    nc.vector.tensor_tensor(
                        hot[:, p], c128[:, C_VOC:C_VOC + P].unsqueeze(1).to_broadcast([P, 2, P]),
                        ids_col[:, bass.ds(2 * n, 2)].unsqueeze(2).to_broadcast([P, 2, P]), ALU.is_equal)\
                      .then_inc(hot_ready, 1)

                def powers(i, more):
                    for p in range(4):
                        n = 4 * i + p
                        dve.wait_ge(squared, n + 3)
                        for half in range(2):
                            lo, k = half * V, NJ - half
                            s = square[lo:lo + V, p % 2]
                            mm = nc.vector.tensor_tensor(
                                mag[lo:lo + V, 0:k, :, bass.ds(2 * n, 2)].rearrange("p j t b -> p b t j"),
                                s[:, :, :, half:NFREQ:2], s[:, :, :, NFREQ + half:NREIM:2], ALU.add)
                        mm.then_inc(summed, 1)
                        if more:
                            one_hots(n + 4, p)

                dve.wait_ge(idcol_ready, 1)
                for p in range(4):
                    one_hots(p, p)
                with dve.Fori(0, NT // 8 - 1) as i:
                    powers(i, True)
                powers(NT // 8 - 1, False)
                dve.wait_ge(ld_emb, 32)
                nc.vector.tensor_copy(emb_high[:, :], emb_raw[:, :]).then_inc(emb_split, 1)
                dve.wait_ge(emb_split, 1)
                nc.vector.scalar_tensor_tensor(out=emb[:, :], in0=emb_high[:, :].bitcast(F32), scalar=c128[:, C_HALF:C_HALF + 1],
                                               in1=emb_raw[:, :], op0=ALU.mult, op1=ALU.add).then_inc(emb_ready, 1)
                dve.wait_ge(spec_done, 1)
                nc.vector.tensor_copy(spec[:, :], bank[0:NT, 7, 0:NFRAME * NSTFT]).then_inc(spec_ready, 1)
                dve.wait_ge(ld_row, 16)
                with dve.Fori(0, NT // 8) as i:
                    for p in range(4):
                        n = 4 * i + p
                        dve.wait_ge(tok_stored, n + 1)
                        nc.vector.tensor_scalar(hot_t[:, p], ids_row[:, bass.ds(2 * P * n, 2 * P)]
                                                .rearrange("p (b l) -> p b l", b=2), c128[:, C_VID:C_VID + 1], None,
                                                ALU.is_equal).then_inc(hot_t_ready, 1)

            @block.scalar
            def _(act):
                for k, name in (("wq1", "L1_attn_Wq"), ("wk1", "L1_attn_Wk"), ("wv1", "L1_attn_Wv")):
                    act.dma_start(m[k][:, :, :], a[name].rearrange("(k p) n -> p k n", p=P)).then_inc(m["ld_" + k], 16)
                act.dma_start(m["wo1"][:, :, :], a["L1_attn_Wo"].rearrange("(n p) d -> p n d", p=P)).then_inc(m["ld_wo1"], 16)
                act.dma_start(m["subln"][:, :], a["L1_attn_subln_w"].unsqueeze(1)).then_inc(m["ld_subln"], 16)
                for k, name in enumerate(("L1_attn_lq1", "L1_attn_lk1", "L1_attn_lq2", "L1_attn_lk2")):
                    act.dma_start(m["lq"][:, k, :], a[name].unsqueeze(0).to_broadcast([P, HD1])).then_inc(m["ld_lq"], 16)
                nc.scalar.preload_act_table(ACT.Sqrt)
                with act.Fori(0, NT // 4) as i:
                    for p in range(2):
                        n = 2 * i + p
                        act.wait_ge(dft_done, n + 1)
                        act.wait_ge(summed, n + 1)
                        nc.scalar.activation(square[:, p].rearrange("p b t c -> p (b t c)"), bank[:, 5 + p, 0:396],
                                             ACT.Square).then_inc(squared, 1)
                act.wait_ge(summed, NT // 2 + 2)
                for j in range(NJ):
                    mm = nc.scalar.activation(mag[:, j], mag[:, j], ACT.Sqrt)
                mm.then_inc(rooted, 1)
                with act.Fori(0, NT // 8) as i:
                    for p in range(4):
                        n = 4 * i + p
                        act.wait_ge(tok_done, n + 1)
                        nc.scalar.copy(h[:, bass.ds(2 * n, 2), :], bank[:, p, :].rearrange("p (b d) -> p b d", b=2))\
                          .then_inc(tok_stored, 1)


def layer0_phase(nc, a, m):
    bank, h, c128 = m["bank"], m["h"], m["c128"]
    ident = c128[:, C_ID:C_ID + P]
    spent = [s.num for s in m["used_sems"]]
    with ExitStack() as ctx:
        def sb(name, shape, dt=F32):
            return ctx.enter_context(nc.sbuf_tensor(name, shape, dt))

        m["used_sems"] = used = []

        def sem(name):
            used.append(ctx.enter_context(nc.semaphore(name)))
            return used[-1]

        w_raw = sb("w_raw", [P, 2, D + 2 * HD0])
        wq = sb("wq", [P, 2, 4, P])
        wk = sb("wk", [P, 2, P])
        wp = sb("wp", [P, 2, D])
        tern_i = sb("tern_i", [P, 2, D], I32)
        tern = sb("tern", [P, 2, D], BF16)
        wt = sb("wt", [P, 2, D], BF16)
        bias = sb("bias0", [P, D])
        scale = sb("scale0", [P, 1])
        rscale = sb("rscale", [P, 1])
        stats = sb("stats", [P, 2, 6])
        meanvar = sb("meanvar", [P, 2, 2])
        rstd = sb("rstd", [P, 2])
        xn = sb("xn", [P, 2, D])
        xnT = sb("xnT", [P, 2, 2, P])
        q_high = sb("q_high", [P, 4, P], F32R)
        qT = sb("qT", [P, 2, 4, P], F32R)
        kT_high = sb("kT_high", [P, 2, 4, P], F32R)
        kT_low = sb("kT_low", [P, 2, 4, P], F32R)
        vone = sb("vone", [P, 2, HD0 + 1])
        negmax = sb("negmax", [P, 4, 4])
        prob = sb("prob", [P, 4, 4, P])
        probT = sb("probT", [P, 2, 4, P])
        rsum = sb("rsum", [P, H0])
        att = sb("att", [P, 2, D])
        attT = sb("attT", [P, 2, 2, P])
        stats2 = sb("stats2", [P, 6])
        meanvar2 = sb("meanvar2", [P, 2])
        rstd2 = sb("rstd2", [P, 1])
        rq = sb("rq", [P, 1])
        xq = sb("xq", [P, D])
        xc = sb("xc", [P, D])
        xi = sb("xi", [P, 2, D], BF16)
        xiT = sb("xiT", [P, 2, 2, P], BF16)

        ld_w, ld_wp, ld_t, ld_b, ld_s = sem("z_ld_w"), sem("z_ld_wp"), sem("z_ld_t"), sem("z_ld_b"), sem("z_ld_s")
        cleared, weights, tern_ready, tern_turned, setup = \
            sem("z_cleared"), sem("z_weights"), sem("z_tern"), sem("z_ternT"), sem("z_setup")
        split, subln_scaled = sem("z_split"), sem("z_subln")
        s_mean, s_rstd, s_xn, s_xnT_ps, s_xnT = \
            sem("z_mean"), sem("z_rstd"), sem("z_xn"), sem("z_xnT_ps"), sem("z_xnT")
        s_q_ps, s_qh, s_q, s_kv_ps, s_kh, s_kv = \
            sem("z_q_ps"), sem("z_qh"), sem("z_q"), sem("z_kv_ps"), sem("z_kh"), sem("z_kv")
        s_score, s_max, s_prob, s_pT_ps, s_pT, s_pv = \
            sem("z_score"), sem("z_max"), sem("z_prob"), sem("z_pT_ps"), sem("z_pT"), sem("z_pv")
        s_rsum, s_att, s_aT_ps, s_aT, s_proj, s_res = \
            sem("z_rsum"), sem("z_att"), sem("z_aT_ps"), sem("z_aT"), sem("z_proj"), sem("z_res")
        s_stat, s_stat2, s_mean2, s_rstd2, s_rq, s_xq, s_xc, s_xi = \
            sem("z_stat"), sem("z_stat2"), sem("z_mean2"), sem("z_rstd2"), sem("z_rq"), sem("z_xq"), sem("z_xc"), sem("z_xi")
        s_xiT_ps, s_xiT, s_ffn, s_bias, s_var, s_var2, s_done = \
            sem("z_xiT_ps"), sem("z_xiT"), sem("z_ffn"), sem("z_bias"), sem("z_var"), sem("z_var2"), sem("z_done")

        BT, BF, BO, BM = 4, 5, 6, 7

        def steps(step, engine):
            def peeled(t):
                step(t, t % 2, lambda lag: 0 <= t - lag < NT)

            for t in range(-2, 4):
                peeled(t)
            with engine.Fori(0, (NT - 6) // 2) as i:
                for p in range(2):
                    step(2 * i + (4 + p), p, lambda lag: True)
            for t in range(NT - 2, NT + 3):
                peeled(t)

        with nc.Block() as block:
            @block.sync
            def _(sp):
                sp.dma_start(w_raw[:, :, :], a["L0_attn_w_attn"].rearrange("(k p) n -> p k n", p=P)).then_inc(ld_w, 16)
                sp.dma_start(tern_i[:, :, :], a["L0_ffn_ternary_weight"].rearrange("(k p) n -> p k n", p=P))\
                  .then_inc(ld_t, 16)
                sp.dma_start(scale[:, :], a["L0_ffn_act_scale"].unsqueeze(0).to_broadcast([P, 1])).then_inc(ld_s, 16)
                sp.dma_start(wp[:, :, :], a["L0_attn_w_proj"].rearrange("(k p) n -> p k n", p=P)).then_inc(ld_wp, 16)
                sp.dma_start(bias[:, :], a["L0_ffn_bias"].unsqueeze(0).to_broadcast([P, D])).then_inc(ld_b, 16)

            @block.gpsimd
            def _(pool):
                nc.gpsimd.sem_clear(range(min(spent), max(spent) + 1))
                nc.gpsimd.memset(kT_high[:, :, :, :].bitcast(F32), 0.0)
                nc.gpsimd.memset(kT_low[:, :, :, :].bitcast(F32), 0.0)
                nc.gpsimd.memset(vone[:, :, :], 1.0).then_inc(cleared, 1)
                pool.wait_ge(ld_b, 16)

                def step(t, p, has):
                    if has(-2):
                        pool.wait_ge(s_var, t + 3)
                        nc.gpsimd.tensor_tensor(rstd[:, p:p + 1], rstd[:, p:p + 1], m["halfneg"][:, 0:1], ALU.pow)\
                          .then_inc(s_rstd, 1)
                    if has(2):
                        pool.wait_ge(s_var2, t - 1)
                        nc.gpsimd.tensor_tensor(rstd2[:, :], rstd2[:, :], m["halfneg"][:, 0:1], ALU.pow)\
                          .then_inc(s_rstd2, 1)
                        pool.wait_ge(s_xq, t - 1)
                        nc.gpsimd.tensor_tensor(h[:, bass.ds(t - 2, 1), :].squeeze(1), h[:, bass.ds(t - 2, 1), :].squeeze(1),
                                                bias[:, :], ALU.add).then_inc(s_bias, 1)
                    if has(2) and not has(3):
                        pool.wait_ge(split, 3)
                        nc.gpsimd.tensor_tensor(m["wv_low"][:, :, :], m["wv1"][:, :, :],
                                                m["wv_high"][:, :, :].bitcast(F32), ALU.subtract)
                    if has(3) and not has(4):
                        nc.gpsimd.tensor_tensor(m["wo_low"][:, :, :], m["wo1"][:, :, :],
                                                m["wo_high"][:, :, :].bitcast(F32), ALU.subtract)

                steps(step, pool)

            @block.tensor
            def _(pe):
                pe.wait_ge(tern_ready, 1)
                for o in range(2):
                    for i in range(2):
                        mm = nc.tensor.transpose(bank[:, BF, 64 * (2 * i + o):64 * (2 * i + o + 1)].bitcast(BF16),
                                                 tern[:, o, i * P:(i + 1) * P], m["identb"][:, :])
                mm.then_inc(tern_turned, 1)
                pe.wait_ge(setup, 1)
                pe.wait_ge(ld_wp, 16)

                def step(t, p, has):
                    q = 1 - p
                    for u in range(4):
                        if has(0):
                            if u == 0:
                                pe.wait_ge(s_q, t + 1)
                                pe.wait_ge(s_kv, t + 1)
                            if has(1):
                                pe.wait_ge(s_prob, 4 * t + u - 3)
                            nc.tensor.matmul(bank[:, u, :].rearrange("p (c k) -> p c k", c=4), m["identb"][:, :],
                                             m["maskb"][:, :].unsqueeze(1).to_broadcast([P, 4, P]),
                                             start=True, stop=False, skip_group_check=True)
                            nc.tensor.matmul(bank[:, u, :], qT[:, p, u, :], kT_low[:, p].rearrange("p r k -> p (r k)"),
                                             start=False, stop=False, skip_group_check=True)
                            mm = nc.tensor.matmul(bank[:, u, :], qT[:, p, u, :], kT_high[:, p].rearrange("p r k -> p (r k)"),
                                                  start=False, stop=True, skip_group_check=True)
                            mm.then_inc(s_score, 1)
                        if has(0) if u >= 3 else has(1):
                            v = (u + 1) % 4
                            n = 4 * t + u - 3
                            pv = p if u == 3 else q
                            pe.wait_ge(s_pT, n + 1)
                            if u == 3 and has(1):
                                pe.wait_ge(s_att, t)
                            for c in range(4):
                                at = (4 * v + c) * (HD0 + 1)
                                mm = nc.tensor.matmul(bank[:, BO, at:at + HD0 + 1], probT[:, v % 2, c, :], vone[:, pv, :],
                                                      start=True, stop=True)
                            mm.then_inc(s_pv, 1)
                        if has(0) if u >= 2 else has(1):
                            v = (u + 2) % 4
                            n = 4 * t + u - 2
                            pe.wait_ge(s_prob, n + 1)
                            if not (u == 2 and not has(1)):
                                pe.wait_ge(s_pT, n)
                            for c in range(4):
                                mm = nc.tensor.transpose(bank[:, BT, c * P:(c + 1) * P], prob[:, v, c, :], ident)
                            mm.then_inc(s_pT_ps, 1)
                        if u == 0:
                            if has(-1):
                                pe.wait_ge(s_xn, t + 2)
                                if has(0):
                                    pe.wait_ge(s_q, t + 1)
                                for k in range(2):
                                    mm = nc.tensor.transpose(bank[:, BF, k * P:(k + 1) * P], xn[:, q, k * P:(k + 1) * P], ident)
                                mm.then_inc(s_xnT_ps, 1)
                            if has(2):
                                pe.wait_ge(s_att, t - 1)
                                if has(-0):
                                    pe.wait_ge(s_kv, t + 1)
                                if has(4):
                                    pe.wait_ge(s_done, t - 3)
                                for k in range(2):
                                    mm = nc.tensor.transpose(bank[:, BM, k * P:(k + 1) * P], att[:, p, k * P:(k + 1) * P], ident)
                                mm.then_inc(s_aT_ps, 1)
                            if has(3):
                                pe.wait_ge(s_xi, t - 2)
                                if not has(-1):
                                    pe.wait_ge(s_xiT, t - 3)
                                for k in range(2):
                                    mm = nc.tensor.transpose(bank[:, BF, D + 64 * k:D + 64 * (k + 1)].bitcast(BF16),
                                                             xi[:, q, k * P:(k + 1) * P], m["identb"][:, :])
                                mm.then_inc(s_xiT_ps, 1)
                        if u == 1 and has(2):
                            pe.wait_ge(s_aT, t - 1)
                            for k in range(2):
                                mm = nc.tensor.matmul(bank[:, BM, 0:D], attT[:, p, k, :], wp[:, k, :],
                                                      start=(k == 0), stop=(k == 1))
                            mm.then_inc(s_proj, 1)
                        if u == 1 and has(-1):
                            pe.wait_ge(s_xnT, t + 2)
                            if has(3):
                                pe.wait_ge(s_xiT, t - 2)
                            for c in range(4):
                                for k in range(2):
                                    mm = nc.tensor.matmul(bank[:, BF, c * P:(c + 1) * P], wq[:, k, c, :], xnT[:, q, k, :],
                                                          start=(k == 0), stop=(k == 1))
                            mm.then_inc(s_q_ps, 1)
                        if u == 2:
                            if has(2):
                                pe.wait_ge(s_res, t - 1)
                            if has(3):
                                pe.wait_ge(s_xiT, t - 2)
                                for k in range(2):
                                    mm = nc.tensor.matmul(bank[:, BM, D:2 * D], xiT[:, q, k, :], wt[:, k, :],
                                                          start=(k == 0), stop=(k == 1))
                                mm.then_inc(s_ffn, 1)
                            if has(-1):
                                for k in range(2):
                                    nc.tensor.matmul(bank[:, BM, 0:P], wk[:, k, :], xnT[:, q, k, :],
                                                     start=(k == 0), stop=(k == 1))
                                for k in range(2):
                                    mm = nc.tensor.matmul(bank[:, BM, P:P + HD0], xnT[:, q, k, :],
                                                          w_raw[:, k, D + HD0:D + 2 * HD0], start=(k == 0), stop=(k == 1))
                                mm.then_inc(s_kv_ps, 1)

                steps(step, pe)

            @block.vector
            def _(dve):
                dve.wait_ge(m["ld_subln"], 16)
                nc.vector.tensor_scalar(m["subln"][:, :], m["subln"][:, :], 1.0 - LAMBDA_INIT, None, ALU.mult)\
                  .then_inc(subln_scaled, 1)
                dve.wait_ge(ld_t, 16)
                nc.vector.tensor_scalar(tern[:, :, :], tern_i[:, :, :], -1.0, None, ALU.add).then_inc(tern_ready, 1)
                dve.wait_ge(cleared, 1)
                dve.wait_ge(ld_w, 16)
                for k in range(2):
                    for c in range(4):
                        for s in range(2):
                            nc.vector.tensor_scalar(
                                wq[:, k, c, :].rearrange("p (r s d) -> p r s d", r=4, s=2)[:, :, s, :],
                                w_raw[:, k, 4 * c * HD0:4 * (c + 1) * HD0].rearrange("p (r d) -> p r d", r=4),
                                HD0 ** -0.5, None, ALU.mult)
                    for r in range(8):
                        nc.vector.tensor_copy(wk[:, k, HD0 * r:HD0 * (r + 1)], w_raw[:, k, D:D + HD0])
                dve.wait_ge(ld_s, 16)
                nc.vector.tensor_scalar(scale[:, :], scale[:, :], 1e-5, 3e38, ALU.max, ALU.min).then_inc(weights, 1)
                dve.wait_ge(weights, 1)
                nc.vector.reciprocal(rscale[:, :], scale[:, :])
                dve.wait_ge(tern_turned, 1)
                nc.vector.tensor_copy(wt[:, :, :], bank[:, BF, 0:256].bitcast(BF16).rearrange("p (k n) -> p k n", k=2))\
                  .then_inc(setup, 1)

                def step(t, p, has):
                    q = 1 - p
                    for u in range(4):
                        if u == 1 and has(-2):
                            dve.wait_ge(s_stat, t + 3)
                        if u == 3 and has(-1):
                            dve.wait_ge(s_kh, t + 2)
                            for r in range(4):
                                at = slice(32 * r, 32 * (r + 1))
                                nc.vector.tensor_tensor(kT_low[at, q, r, :], bank[at, BM, 0:P],
                                                        kT_high[at, q, r, :].bitcast(F32), ALU.subtract)
                            nc.vector.tensor_copy(vone[:, q, 0:HD0], bank[:, BM, P:P + HD0]).then_inc(s_kv, 1)
                        if has(0):
                            dve.wait_ge(s_score, 4 * t + u + 1)
                            nc.vector.tensor_reduce(negmax[:, u, :], bank[:, u, :].rearrange("p (c k) -> p c k", c=4),
                                                    AX.X, ALU.max, negate=True).then_inc(s_max, 1)
                        if u == 0:
                            if has(2):
                                dve.wait_ge(s_aT_ps, t - 1)
                                nc.vector.tensor_copy(attT[:, p], bank[:, BM, 0:D].rearrange("p (k n) -> p k n", k=2))\
                                  .then_inc(s_aT, 1)
                            if has(-2):
                                nc.vector.bn_stats(stats[:, p, :], h[:, bass.ds(t + 2, 1), :].squeeze(1)).then_inc(s_stat, 1)
                        if u == 1:
                            if has(3):
                                dve.wait_ge(s_xiT_ps, t - 2)
                            if has(-1):
                                dve.wait_ge(s_xnT_ps, t + 2)
                                nc.vector.tensor_copy(xnT[:, q], bank[:, BF, 0:D].rearrange("p (k n) -> p k n", k=2))\
                                  .then_inc(s_xnT, 1)
                            if has(3):
                                nc.vector.tensor_copy(xiT[:, q], bank[:, BF, D:D + P].bitcast(BF16)
                                                      .rearrange("p (k n) -> p k n", k=2)).then_inc(s_xiT, 1)
                            if has(-2):
                                nc.vector.bn_aggr(meanvar[:, p, :], stats[:, p, :]).then_inc(s_mean, 1)
                                dve.wait_ge(s_mean, t + 3)
                                nc.vector.tensor_scalar(rstd[:, p:p + 1], meanvar[:, p, 1:2], EPS, None, ALU.add)\
                                  .then_inc(s_var, 1)
                        if u == 2:
                            o = bank[:, BO, 0:H0 * (HD0 + 1)].rearrange("p (n d) -> p n d", n=H0)
                            if has(2):
                                dve.wait_ge(s_proj, t - 1)
                                ht = h[:, bass.ds(t - 2, 1), :].squeeze(1)
                                nc.vector.tensor_tensor(ht, ht, bank[:, BM, 0:D], ALU.add).then_inc(s_res, 1)
                            if has(1):
                                dve.wait_ge(s_pv, 4 * t)
                                nc.vector.reciprocal(rsum[:, :], o[:, :, HD0]).then_inc(s_rsum, 1)
                            if has(2):
                                dve.wait_ge(s_res, t - 1)
                            if has(1):
                                dve.wait_ge(s_rsum, t)
                                nc.vector.tensor_tensor(att[:, q].rearrange("p (n d) -> p n d", n=H0), o[:, :, 0:HD0],
                                                        rsum[:, :].unsqueeze(2).to_broadcast([P, H0, HD0]), ALU.mult)\
                                  .then_inc(s_att, 1)
                            if has(2):
                                nc.vector.bn_stats(stats2[:, :], ht).then_inc(s_stat2, 1)
                                dve.wait_ge(s_stat2, t - 1)
                            if has(-1):
                                dve.wait_ge(s_qh, t + 2)
                                nc.vector.scalar_tensor_tensor(
                                    out=qT[:, q].rearrange("p c n -> p (c n)"),
                                    in0=q_high[:, :, :].rearrange("p c n -> p (c n)").bitcast(F32),
                                    scalar=c128[:, C_LOW:C_LOW + 1], in1=bank[:, BF, :], op0=ALU.mult, op1=ALU.add)\
                                  .then_inc(s_q, 1)
                            if has(2):
                                nc.vector.bn_aggr(meanvar2[:, :], stats2[:, :]).then_inc(s_mean2, 1)
                                dve.wait_ge(s_mean2, t - 1)
                                nc.vector.tensor_scalar(rstd2[:, :], meanvar2[:, 1:2], EPS, None, ALU.add).then_inc(s_var2, 1)
                        if u == 3:
                            if has(3):
                                dve.wait_ge(s_ffn, t - 2)
                                dve.wait_ge(s_bias, t - 2)
                                ht = h[:, bass.ds(t - 3, 1), :].squeeze(1)
                                nc.vector.scalar_tensor_tensor(out=ht, in0=bank[:, BM, D:2 * D], scalar=scale[:, 0:1],
                                                               in1=ht, op0=ALU.mult, op1=ALU.add).then_inc(s_done, 1)
                            if has(-2):
                                dve.wait_ge(s_rstd, t + 3)
                                nc.vector.tensor_scalar(xn[:, p], h[:, bass.ds(t + 2, 1), :].squeeze(1),
                                                        meanvar[:, p, 0:1], rstd[:, p:p + 1], ALU.subtract, ALU.mult)\
                                  .then_inc(s_xn, 1)
                            if has(2):
                                dve.wait_ge(s_rstd2, t - 1)
                                nc.vector.tensor_scalar(xq[:, :], h[:, bass.ds(t - 2, 1), :].squeeze(1),
                                                        meanvar2[:, 0:1], rstd2[:, 0:1], ALU.subtract, ALU.mult)\
                                  .then_inc(s_xq, 1)
                                dve.wait_ge(s_xq, t - 1)
                                nc.vector.tensor_scalar(xc[:, :], xq[:, :], rscale[:, 0:1], 127.0, ALU.mult, ALU.min)\
                                  .then_inc(s_xc, 1)
                                dve.wait_ge(s_xc, t - 1)
                                nc.vector.tensor_scalar(xq[:, :], xc[:, :], -127.0, ROUND, ALU.max, ALU.add).then_inc(s_rq, 1)
                                dve.wait_ge(s_rq, t - 1)
                                nc.vector.tensor_scalar(xi[:, p], xq[:, :], -ROUND, None, ALU.add).then_inc(s_xi, 1)

                steps(step, dve)

            @block.scalar
            def _(act):
                nc.scalar.preload_act_table(ACT.Exp)
                act.wait_ge(m["ld_wq1"], 16)
                nc.scalar.mul(m["wq1"][:, :, :], m["wq1"][:, :, :], HD1 ** -0.5)
                act.wait_ge(m["ld_wv1"], 16)
                nc.scalar.copy(m["wv_high"][:, :, :], m["wv1"][:, :, :]).then_inc(split, 1)
                act.wait_ge(m["ld_wo1"], 16)
                act.wait_ge(subln_scaled, 1)
                nc.scalar.mul(m["wo1"][:, :, :], m["wo1"][:, :, :], m["subln"][:, 0:1]).then_inc(split, 1)
                act.wait_ge(split, 2)
                nc.scalar.copy(m["wo_high"][:, :, :], m["wo1"][:, :, :]).then_inc(split, 1)

                def step(t, p, has):
                    q = 1 - p
                    for u in range(4):
                        if u == 2 and has(-1):
                            act.wait_ge(s_q_ps, t + 2)
                            if has(0):
                                act.wait_ge(s_q, t + 1)
                            nc.scalar.copy(q_high[:, :, :], bank[:, BF, :].rearrange("p (c n) -> p c n", c=4))\
                              .then_inc(s_qh, 1)
                        if has(0) if u >= 2 else has(1):
                            n = 4 * t + u - 2
                            act.wait_ge(s_pT_ps, n + 1)
                            nc.scalar.copy(probT[:, u % 2], bank[:, BT, :].rearrange("p (c n) -> p c n", c=4))\
                              .then_inc(s_pT, 1)
                        if u == 2 and has(-1):
                            act.wait_ge(s_kv_ps, t + 2)
                            for r in range(4):
                                at = slice(32 * r, 32 * (r + 1))
                                mm = nc.scalar.copy(kT_high[at, q, r, :], bank[at, BM, 0:P])
                            mm.then_inc(s_kh, 1)
                        if has(0):
                            act.wait_ge(s_max, 4 * t + u + 1)
                            for c in range(4):
                                mm = nc.scalar.activation(prob[:, u, c, :], bank[:, u, c * P:(c + 1) * P], ACT.Exp,
                                                          bias=negmax[:, u, c:c + 1])
                            mm.then_inc(s_prob, 1)

                steps(step, act)


def layer1_phase(nc, a, m, rows, out):
    bank, h, c128 = m["bank"], m["h"], m["c128"]
    ident = c128[:, C_ID:C_ID + P]
    wq, wk, lq = m["wq1"], m["wk1"], m["lq"]
    wv_high, wv_low, wo_high, wo_low = m["wv_high"], m["wv_low"], m["wo_high"], m["wo_low"]
    spent = [s.num for s in m["used_sems"]]
    with ExitStack() as ctx:
        def sb(name, shape, dt=F32):
            return ctx.enter_context(nc.sbuf_tensor(name, shape, dt))

        def sem(name):
            return ctx.enter_context(nc.semaphore(name))

        wg = sb("wg", [P, 2, NE])
        bg = sb("bg", [P, NE])
        ones = sb("ones", [P, P], BF16)
        below = sb("below", [P, P], BF16)
        blank = sb("blank", [P, ROW])
        lprod = sb("lprod", [P, 2, HD1])
        lsum = sb("lsum", [P, 2])
        lexp = sb("lexp", [P, 2])
        neglam = sb("neglam", [P, 1])
        xn = sb("xn1", [P, 2, D])
        xnT = sb("xnT1", [P, 2, 2, P])
        xnT_high, xnT_low = sb("xnT_high", [P, 2, 2, P], F32R), sb("xnT_low", [P, 2, 2, P], F32R)
        qT = sb("qT1", [P, 2, H1, P])
        kT = sb("kT1", [P, 2, H1, P])
        val = sb("val1", [P, 2, H1 * P])
        stats = sb("stats1", [P, 6])
        meanvar = sb("meanvar1", [P, 2])
        rstd = sb("rstd1", [P, 1])
        negmax = sb("negmax1", [P, 2, 8])
        prob = sb("prob1", [P, 2, 8, P])
        psum_ = sb("psum1", [P, 2, 8])
        rsec = sb("rsec", [P, 4])
        ratio = sb("ratio", [P, 4])
        epsum = sb("epsum", [P, 2, 4])
        diff = sb("diff", [P, 2, 4, P])
        diffT = sb("diffT", [P, 2, 4, P])
        junk = sb("junk", [P, 2, 4, P])
        ssq = sb("ssq", [P, 2, 4])
        meansq = sb("meansq", [P, 2, 4])
        normed = sb("normed", [P, 2, 4, P])
        normedT_high, normedT_low = sb("normedT_high", [P, 2, 4, P], F32R), sb("normedT_low", [P, 2, 4, P], F32R)
        gstats = sb("gstats", [P, 6])
        gmeanvar = sb("gmeanvar", [P, 2])
        grstd = sb("grstd", [P, 1])
        gn = sb("gn", [P, D])
        gnT = sb("gnT", [P, 2, P])
        logit = sb("logit", [P, NE])
        glmax = sb("glmax", [P, 1])
        gnegmax = sb("gnegmax", [P, 1])
        gexp = sb("gexp", [P, NE])
        gsum = sb("gsum", [P, 1])
        top = sb("top", [P, NE])
        cand = sb("cand", [P, NE])
        first = sb("first", [P, 1])
        hot = sb("hot1", [P, NE], BF16)
        hotsum = sb("hotsum", [P, NE], BF16)
        posjunk = sb("posjunk", [P, NE])
        pos = sb("pos", [P, 1])
        over = sb("over", [P, 1])
        slotf = sb("slotf", [P, 1])
        slot = sb("slot", [P, 2], U32)
        row = sb("row", [P, 2, ROW])

        ld_wg, ld_bg = sem("y_ld_wg"), sem("y_ld_bg")
        blanked, blank_ready, setup_pool, setup_dve = sem("y_blanked"), sem("y_blank"), sem("y_setup_pool"), sem("y_setup_dve")
        s_lprod, s_lsum, s_lexp, s_lam = sem("y_lprod"), sem("y_lsum"), sem("y_lexp"), sem("y_lam")
        s_stat, s_mean, s_var, s_rstd, s_xn, s_xnT_ps, s_xnT = \
            sem("y_stat"), sem("y_mean"), sem("y_var"), sem("y_rstd"), sem("y_xn"), sem("y_xnT_ps"), sem("y_xnT")
        s_fill, s_fa, s_fd = sem("y_fill"), sem("y_fill_act"), sem("y_fill_dve")
        s_score, s_max, s_exp = sem("y_score"), sem("y_max"), sem("y_exp")
        s_rsec, s_ratio, s_diff, s_dT_ps, s_dT = sem("y_rsec"), sem("y_ratio"), sem("y_diff"), sem("y_dT_ps"), sem("y_dT")
        s_pv, s_sq, s_msq, s_fac, s_norm, s_nT_ps, s_nT_high, s_nT = \
            sem("y_pv"), sem("y_sq"), sem("y_msq"), sem("y_fac"), sem("y_norm"), sem("y_nT_ps"), sem("y_nTh"), sem("y_nT")
        s_x_high, s_x_low = sem("y_xnTh"), sem("y_xnTl")
        s_eps, s_wo, s_res = sem("y_eps"), sem("y_wo"), sem("y_res")
        g_stat, g_mean, g_var, g_rstd, g_norm, g_T_ps, g_T = \
            sem("g_stat"), sem("g_mean"), sem("g_var"), sem("g_rstd"), sem("g_norm"), sem("g_T_ps"), sem("g_T")
        g_lg_ps, g_lg, g_max, g_neg, g_exp, g_gate, g_top, g_cand, g_first, g_hot = \
            sem("g_lg_ps"), sem("g_lg"), sem("g_max"), sem("g_neg"), sem("g_exp"), sem("g_gate"), sem("g_top"), \
            sem("g_cand"), sem("g_first"), sem("g_hot")
        g_ps, g_pos, g_sum, g_over, g_slotf, g_slot, g_row = \
            sem("g_ps"), sem("g_pos"), sem("g_sum"), sem("g_over"), sem("g_slotf"), sem("g_slot"), sem("g_row")

        BD, BV, BX, BP = 4, 5, 6, 7

        def steps(step, engine):
            def peeled(t):
                step(t, t % 2, lambda lag: 0 <= t - lag < NT)

            for t in range(-3, 4):
                peeled(t)
            with engine.Fori(0, (NT - 8) // 2) as i:
                for p in range(2):
                    step(2 * i + (4 + p), p, lambda lag: True)
            for t in range(NT - 4, NT + 4):
                peeled(t)

        with nc.Block() as block:
            @block.sync
            def _(sp):
                sp.dma_start(wg[:, :, :], a["L1_ffn_Wg"].rearrange("(k p) n -> p k n", p=P)).then_inc(ld_wg, 16)
                sp.dma_start(bg[:, :], a["L1_ffn_bg"].unsqueeze(0).to_broadcast([P, NE])).then_inc(ld_bg, 16)
                sp.wait_ge(blank_ready, 2)
                sp.dma_start(rows.rearrange("(s p) c -> p s c", p=P),
                             blank[:, :].unsqueeze(1).to_broadcast([P, NT, ROW])).then_inc(blanked, 16)

                def step(t, p, has):
                    if has(1):
                        sp.wait_ge(s_res, t)
                        sp.dma_start(out[bass.ds(P * (t - 1), P), :], h[:, bass.ds(t - 1, 1), :].squeeze(1))\
                          .then_inc(m["prefilled"], 16)

                steps(step, sp)

            @block.gpsimd
            def _(pool):
                nc.gpsimd.sem_clear(range(min(spent), max(spent) + 1))
                nc.gpsimd.memset(ones[:, :], 1.0)
                nc.gpsimd.memset(hotsum[:, :], 0.0).then_inc(setup_pool, 1)
                nc.gpsimd.memset(blank[:, :], 0.0).then_inc(blank_ready, 1)
                pool.wait_ge(blank_ready, 1)
                nc.gpsimd.memset(blank[:, D:D + 1], NOWHERE).then_inc(blank_ready, 1)
                last_row = pool.to_reg(NE * CAP - 1)

                def power(ap, done):
                    nc.gpsimd.tensor_tensor(ap, ap, m["halfneg"][:, 0:ap.shape[1]], ALU.pow).then_inc(done, 1)

                def step(t, p, has):
                    if has(1):
                        pool.wait_ge(s_msq, 2 * t - 1)
                        power(meansq[:, 0, :], s_fac)
                    if has(2):
                        pool.wait_ge(g_var, t - 1)
                        power(grstd[:, :], g_rstd)
                    if has(4):
                        pool.wait_ge(g_row, t - 3)
                        pool.wait_ge(g_gate, t - 3)
                        pool.wait_ge(g_slot, t - 3)
                    if has(-3):
                        pool.wait_ge(s_var, t + 4)
                        power(rstd[:, :], s_rstd)
                    if has(4):
                        nc.gpsimd.indirect_dma_start(
                            out=rows, out_offset=bass.IndirectOffsetOnAxis(ap=slot[:, p:p + 1], axis=0),
                            in_=row[:, p, :], in_offset=None, bounds_check=last_row, oob_is_err=False)\
                          .then_inc(m["scattered"][p], 16)
                    if has(1):
                        pool.wait_ge(s_msq, 2 * t)
                        power(meansq[:, 1, :], s_fac)
                    if has(3) and not has(4):
                        pool.wait_ge(blanked, 16)
                    if has(3):
                        q = 1 - p
                        if has(5):
                            pool.wait_ge(m["scattered"][q], 8 * (t - 3 - q))
                        nc.gpsimd.tensor_copy(row[:, q, 0:D], h[:, bass.ds(t - 3, 1), :].squeeze(1))
                        nc.gpsimd.tensor_copy(row[:, q, D:D + 1], c128[:, bass.ds(C_TOK + t - 3, 1)]).then_inc(g_row, 1)

                    if has(-2):
                        pool.wait_ge(s_x_high, t + 3)
                        nc.gpsimd.tensor_tensor(xnT_low[:, p], xnT[:, p], xnT_high[:, p].bitcast(F32), ALU.subtract)\
                          .then_inc(s_x_low, 1)

                steps(step, pool)

            @block.tensor
            def _(pe):
                pe.wait_ge(setup_pool, 1)
                pe.wait_ge(setup_dve, 1)
                pe.wait_ge(ld_wg, 16)
                pe.wait_ge(m["ld_wk1"], 16)
                pe.wait_ge(m["ld_wv1"], 16)

                def fill(t, j, par):
                    if j == 0:
                        pe.wait_ge(s_xnT, t + 1)
                    if j < 4:
                        w = (wq, wk)[j // 2]
                        for c in range(4):
                            n = 4 * (j % 2) + c
                            for k in range(2):
                                mm = nc.tensor.matmul(bank[:, BP, c * P:(c + 1) * P], w[:, k, n * P:(n + 1) * P],
                                                      xnT[:, par, k, :], start=(k == 0), stop=(k == 1))
                    else:
                        if j == 4:
                            pe.wait_ge(s_x_low, t + 1)
                        at = slice(512 * (j - 4), 512 * (j - 3))
                        for k in range(2):
                            nc.tensor.matmul(bank[:, BP, :], xnT_low[:, par, k, :], wv_high[:, k, at],
                                             start=(k == 0), stop=False)
                            nc.tensor.matmul(bank[:, BP, :], xnT_high[:, par, k, :], wv_low[:, k, at],
                                             start=False, stop=False)
                            mm = nc.tensor.matmul(bank[:, BP, :], xnT_high[:, par, k, :], wv_high[:, k, at],
                                                  start=False, stop=(k == 1))
                    mm.then_inc(s_fill, 1)

                def scores(q, p):
                    for c in range(4):
                        n = 4 * q + c
                        for s in range(2):
                            mm = nc.tensor.matmul(bank[:, 2 * q + s, c * P:(c + 1) * P], qT[64 * s:64 * s + 64, p, n, :],
                                                  kT[64 * s:64 * s + 64, p, n, :], start=True, stop=True)
                    mm.then_inc(s_score, 1)

                def turn(src, b, done):
                    for c in range(4):
                        mm = nc.tensor.transpose(bank[:, b, c * P:(c + 1) * P], src[:, c, :], ident)
                    mm.then_inc(done, 1)

                def outputs(q, par):
                    for c in range(4):
                        n = 4 * q + c
                        mm = nc.tensor.matmul(bank[:, BV, c * P:(c + 1) * P], diffT[:, q, c, :],
                                              val[:, par, n * P:(n + 1) * P], start=True, stop=True)
                    mm.then_inc(s_pv, 1)

                def step(t, p, has):
                    o = 1 - p
                    if has(0):
                        pe.wait_ge(s_fa, 4 * t + 3)
                        if has(1):
                            pe.wait_ge(s_exp, 2 * t - 1)
                        scores(0, p)
                    if has(-1):
                        if has(0):
                            pe.wait_ge(s_fd, 2 * t + 2)
                        fill(t + 1, 0, o)
                    if has(1):
                        pe.wait_ge(s_diff, 2 * t)
                        if has(3):
                            pe.wait_ge(g_lg, t - 2)
                        turn(diff[:, 1], BD, s_dT_ps)
                    if has(1):
                        pe.wait_ge(s_norm, 2 * t - 1)
                        if has(2):
                            pe.wait_ge(s_res, t - 1)
                        turn(normed[:, 0], BX, s_nT_ps)
                    if has(-1):
                        pe.wait_ge(s_fa, 4 * t + 5)
                        fill(t + 1, 1, o)
                    if has(1):
                        pe.wait_ge(s_dT, 2 * t)
                        pe.wait_ge(s_fd, 2 * t)
                        pe.wait_ge(s_norm, 2 * t - 1)
                        outputs(1, o)
                    if has(-2):
                        pe.wait_ge(s_xn, t + 3)
                        for k in range(2):
                            mm = nc.tensor.transpose(bank[:, BD, k * P:(k + 1) * P], xn[:, p, k * P:(k + 1) * P], ident)
                        mm.then_inc(s_xnT_ps, 1)
                    if has(-1):
                        pe.wait_ge(s_fa, 4 * t + 6)
                        fill(t + 1, 2, o)
                    if has(3):
                        pe.wait_ge(g_hot, t - 2)
                        if has(-2):
                            pe.wait_ge(s_xnT, t + 3)
                        if has(4):
                            pe.wait_ge(g_sum, t - 3)
                        nc.tensor.matmul(bank[:, BD, D:D + NE], below[:, :], hot[:, :], start=True, stop=False)
                        nc.tensor.matmul(bank[:, BD, D:D + NE], ones[:, :], hotsum[:, :], start=False, stop=True)\
                          .then_inc(g_ps, 1)
                    if has(2):
                        pe.wait_ge(g_norm, t - 1)
                        if has(1):
                            pe.wait_ge(s_nT, 2 * t - 1)
                        else:
                            pe.wait_ge(s_res, t - 1)
                        for k in range(2):
                            mm = nc.tensor.transpose(bank[:, BX, k * P:(k + 1) * P], gn[:, k * P:(k + 1) * P], ident)
                        mm.then_inc(g_T_ps, 1)
                    if has(0):
                        pe.wait_ge(s_fd, 2 * t + 1)
                        if has(1):
                            pe.wait_ge(s_exp, 2 * t)
                        scores(1, p)
                    if has(-1):
                        pe.wait_ge(s_fa, 4 * t + 7)
                        fill(t + 1, 3, o)
                    if has(1):
                        pe.wait_ge(s_norm, 2 * t)
                        if has(2):
                            pe.wait_ge(g_T, t - 1)
                        turn(normed[:, 1], BX, s_nT_ps)
                    if has(0):
                        pe.wait_ge(s_diff, 2 * t + 1)
                        if has(-2):
                            pe.wait_ge(s_xnT, t + 3)
                        if has(3):
                            pe.wait_ge(g_pos, t - 2)
                        turn(diff[:, 0], BD, s_dT_ps)
                    if has(-1):
                        pe.wait_ge(s_fd, 2 * t + 3)
                        fill(t + 1, 4, o)
                    if has(1):
                        pe.wait_ge(s_nT, 2 * t)
                        for n in range(H1):
                            nc.tensor.matmul(bank[:, BX, 0:D], normedT_low[:, n // 4, n % 4, :], wo_high[:, n, :],
                                             start=(n == 0), stop=False)
                            nc.tensor.matmul(bank[:, BX, 0:D], normedT_high[:, n // 4, n % 4, :], wo_low[:, n, :],
                                             start=False, stop=False)
                            mm = nc.tensor.matmul(bank[:, BX, 0:D], normedT_high[:, n // 4, n % 4, :], wo_high[:, n, :],
                                                  start=False, stop=(n == H1 - 1))
                        mm.then_inc(s_wo, 1)
                    if has(2):
                        pe.wait_ge(g_T, t - 1)
                        if has(0):
                            pe.wait_ge(s_dT, 2 * t + 1)
                        elif has(3):
                            pe.wait_ge(g_pos, t - 2)
                        for k in range(2):
                            mm = nc.tensor.matmul(bank[:, BD, 0:NE], gnT[:, k, :], wg[:, k, :], start=(k == 0), stop=(k == 1))
                        mm.then_inc(g_lg_ps, 1)
                    if has(-1):
                        pe.wait_ge(s_fa, 4 * t + 8)
                        fill(t + 1, 5, o)
                    if has(0):
                        pe.wait_ge(s_dT, 2 * t + 1)
                        pe.wait_ge(s_fa, 4 * t + 4)
                        if has(1):
                            pe.wait_ge(s_norm, 2 * t)
                        outputs(0, p)

                steps(step, pe)

            @block.vector
            def _(dve):
                dve.wait_ge(m["ld_lq"], 64)
                nc.vector.tensor_tensor(lprod[:, :, :], lq[:, 0:4:2, :], lq[:, 1:4:2, :], ALU.mult).then_inc(s_lprod, 1)
                dve.wait_ge(s_lprod, 1)
                nc.vector.tensor_reduce(lsum[:, :], lprod[:, :, :], AX.X, ALU.add).then_inc(s_lsum, 1)
                nc.vector.tensor_copy(below[:, :], c128[:, C_TRI:C_TRI + P])
                dve.wait_ge(s_lexp, 1)
                nc.vector.tensor_tensor(neglam[:, :], lexp[:, 1:2], lexp[:, 0:1], ALU.subtract).then_inc(s_lam, 1)
                dve.wait_ge(s_lam, 1)
                nc.vector.tensor_scalar(neglam[:, :], neglam[:, :], -LAMBDA_INIT, None, ALU.add).then_inc(setup_dve, 1)
                dve.wait_ge(setup_dve, 1)
                dve.wait_ge(ld_bg, 16)

                def quad(ap):
                    return ap.rearrange("p (c n) -> p c n", c=4)

                def take(j, t, par):
                    dve.wait_ge(s_fill, 6 * t + j + 1)
                    if j < 4:
                        dst = (qT, kT)[j // 2][:, par, 4 * (j % 2):4 * (j % 2) + 4, :]
                        nc.vector.tensor_copy(dst, quad(bank[:, BP, :])).then_inc(s_fd, 1)
                    else:
                        nc.vector.tensor_copy(val[:, par, 512 * (j - 4):512 * (j - 3)], bank[:, BP, :]).then_inc(s_fd, 1)

                def maxima(n, q):
                    dve.wait_ge(s_score, n + 1)
                    nc.vector.tensor_reduce(negmax[:, q, :], bank[:, 2 * q:2 * q + 2, :].rearrange("p s (c k) -> p (s c) k", c=4),
                                            AX.X, ALU.max, negate=True).then_inc(s_max, 1)

                def normed_low(n, q):
                    dve.wait_ge(s_nT_high, n + 1)
                    nc.vector.tensor_tensor(normedT_low[:, q], quad(bank[:, BX, :]), normedT_high[:, q].bitcast(F32),
                                            ALU.subtract).then_inc(s_nT, 1)

                def mean_square(n, q):
                    dve.wait_ge(s_sq, n + 1)
                    nc.vector.scalar_tensor_tensor(out=meansq[:, q, :], in0=ssq[:, q, :], scalar=1.0 / P, in1=epsum[:, q, :],
                                                   op0=ALU.mult, op1=ALU.add).then_inc(s_msq, 1)

                def normalise(n, q):
                    dve.wait_ge(s_fac, n + 1)
                    nc.vector.tensor_tensor(normed[:, q], quad(bank[:, BV, :]),
                                            meansq[:, q, :].unsqueeze(2).to_broadcast([P, 4, P]), ALU.mult).then_inc(s_norm, 1)

                def combine(n, q):
                    dve.wait_ge(s_exp, n + 1)
                    nc.vector.reciprocal(rsec[:, :], psum_[:, q, 4:8]).then_inc(s_rsec, 1)
                    nc.vector.scalar_tensor_tensor(out=epsum[:, q, :], in0=psum_[:, q, 0:4], scalar=EPS,
                                                   in1=psum_[:, q, 0:4], op0=ALU.mult, op1=ALU.mult)
                    dve.wait_ge(s_rsec, n + 1)
                    nc.vector.scalar_tensor_tensor(out=ratio[:, :], in0=psum_[:, q, 0:4], scalar=neglam[:, 0:1],
                                                   in1=rsec[:, :], op0=ALU.mult, op1=ALU.mult).then_inc(s_ratio, 1)
                    dve.wait_ge(s_ratio, n + 1)
                    for c in range(4):
                        mm = nc.vector.scalar_tensor_tensor(out=diff[:, q, c, :], in0=prob[:, q, 4 + c, :],
                                                            scalar=ratio[:, c:c + 1], in1=prob[:, q, c, :],
                                                            op0=ALU.mult, op1=ALU.add)
                    mm.then_inc(s_diff, 1)

                def step(t, p, has):
                    o = 1 - p
                    if has(3):
                        dve.wait_ge(g_lg_ps, t - 2)
                        nc.vector.tensor_tensor(logit[:, :], bank[:, BD, 0:NE], bg[:, :], ALU.add).then_inc(g_lg, 1)
                    if has(1):
                        combine(2 * t - 1, 1)
                    if has(2):
                        dve.wait_ge(s_res, t - 1)
                    if has(1):
                        mean_square(2 * t - 2, 0)
                    if has(2):
                        nc.vector.bn_stats(gstats[:, :], h[:, bass.ds(t - 2, 1), :].squeeze(1)).then_inc(g_stat, 1)
                        dve.wait_ge(g_stat, t - 1)
                    if has(0):
                        maxima(2 * t, 0)
                    if has(2):
                        nc.vector.bn_aggr(gmeanvar[:, :], gstats[:, :]).then_inc(g_mean, 1)
                    if has(1):
                        normalise(2 * t - 2, 0)
                    if has(2):
                        dve.wait_ge(g_mean, t - 1)
                        nc.vector.tensor_scalar(grstd[:, :], gmeanvar[:, 1:2], EPS, None, ALU.add).then_inc(g_var, 1)
                    if has(-3):
                        nc.vector.bn_stats(stats[:, :], h[:, bass.ds(t + 3, 1), :].squeeze(1)).then_inc(s_stat, 1)
                    if has(2):
                        dve.wait_ge(g_rstd, t - 1)
                        nc.vector.tensor_scalar(gn[:, :], h[:, bass.ds(t - 2, 1), :].squeeze(1), gmeanvar[:, 0:1],
                                                grstd[:, 0:1], ALU.subtract, ALU.mult).then_inc(g_norm, 1)
                    if has(-3):
                        dve.wait_ge(s_stat, t + 4)
                    if has(1):
                        dve.wait_ge(s_dT_ps, 2 * t)
                        nc.vector.tensor_copy(diffT[:, 1], quad(bank[:, BD, :])).then_inc(s_dT, 1)
                    if has(-3):
                        nc.vector.bn_aggr(meanvar[:, :], stats[:, :]).then_inc(s_mean, 1)
                        dve.wait_ge(s_mean, t + 4)
                        nc.vector.tensor_scalar(rstd[:, :], meanvar[:, 1:2], EPS, None, ALU.add).then_inc(s_var, 1)
                    if has(3):
                        dve.wait_ge(g_lg, t - 2)
                        nc.vector.tensor_reduce(glmax[:, :], logit[:, :], AX.X, ALU.max).then_inc(g_max, 1)
                        dve.wait_ge(g_max, t - 2)
                        nc.vector.tensor_scalar(gnegmax[:, :], glmax[:, :], -1.0, None, ALU.mult).then_inc(g_neg, 1)
                        nc.vector.tensor_scalar(top[:, :], logit[:, :], glmax[:, 0:1], None, ALU.is_equal).then_inc(g_top, 1)
                        dve.wait_ge(g_top, t - 2)
                        nc.vector.scalar_tensor_tensor(out=cand[:, :], in0=top[:, :], scalar=-64.0,
                                                       in1=c128[:, C_EXP:C_EXP + NE], op0=ALU.mult, op1=ALU.add).then_inc(g_cand, 1)
                        dve.wait_ge(g_cand, t - 2)
                        nc.vector.tensor_reduce(first[:, :], cand[:, :], AX.X, ALU.min).then_inc(g_first, 1)
                        dve.wait_ge(g_first, t - 2)
                        nc.vector.tensor_scalar(hot[:, :], cand[:, :], first[:, 0:1], None, ALU.is_equal).then_inc(g_hot, 1)
                    if has(-2):
                        dve.wait_ge(s_xnT_ps, t + 3)
                        nc.vector.tensor_copy(xnT[:, p], bank[:, BD, 0:D].rearrange("p (k n) -> p k n", k=2)).then_inc(s_xnT, 1)
                    if has(1):
                        normed_low(2 * t - 2, 0)
                    if has(0):
                        combine(2 * t, 0)
                    if has(1):
                        mean_square(2 * t - 1, 1)
                    if has(1):
                        normalise(2 * t - 1, 1)
                    if has(3):
                        dve.wait_ge(g_ps, t - 2)
                        nc.vector.scalar_tensor_tensor(out=posjunk[:, :], in0=bank[:, BD, D:D + NE], scalar=1.0,
                                                       in1=hot[:, :], op0=ALU.mult, op1=ALU.mult,
                                                       accum_out=pos[:, :]).then_inc(g_pos, 1)
                    if has(0):
                        maxima(2 * t + 1, 1)
                    if has(2):
                        dve.wait_ge(g_T_ps, t - 1)
                        nc.vector.tensor_copy(gnT[:, :, :], bank[:, BX, 0:D].rearrange("p (k n) -> p k n", k=2)).then_inc(g_T, 1)
                    if has(-1):
                        take(3, t + 1, o)
                    if has(3):
                        nc.vector.tensor_tensor(hotsum[:, :], hotsum[:, :], hot[:, :], ALU.add).then_inc(g_sum, 1)
                        dve.wait_ge(g_pos, t - 2)
                        nc.vector.tensor_scalar(over[:, :], pos[:, :], float(CAP), NOWHERE, ALU.is_ge, ALU.mult).then_inc(g_over, 1)
                        nc.vector.scalar_tensor_tensor(out=slotf[:, :], in0=first[:, :], scalar=float(CAP), in1=pos[:, :],
                                                       op0=ALU.mult, op1=ALU.add).then_inc(g_slotf, 1)
                        dve.wait_ge(g_slotf, t - 2)
                        dve.wait_ge(g_over, t - 2)
                        if has(5):
                            dve.wait_ge(m["scattered"][o], 8 * (t - 3 - o))
                        nc.vector.scalar_tensor_tensor(out=slot[:, o:o + 1], in0=slotf[:, :], scalar=64.0 * CAP,
                                                       in1=over[:, :], op0=ALU.add, op1=ALU.add).then_inc(g_slot, 1)
                    if has(-3):
                        dve.wait_ge(s_rstd, t + 4)
                        nc.vector.tensor_scalar(xn[:, o], h[:, bass.ds(t + 3, 1), :].squeeze(1), meanvar[:, 0:1],
                                                rstd[:, 0:1], ALU.subtract, ALU.mult).then_inc(s_xn, 1)
                    if has(1):
                        normed_low(2 * t - 1, 1)
                    if has(0):
                        dve.wait_ge(s_dT_ps, 2 * t + 1)
                        nc.vector.tensor_copy(diffT[:, 0], quad(bank[:, BD, :])).then_inc(s_dT, 1)
                    if has(3):
                        dve.wait_ge(g_exp, t - 2)
                        nc.vector.reciprocal(row[:, o, D + 1:D + 2], gsum[:, :]).then_inc(g_gate, 1)
                    if has(1):
                        dve.wait_ge(s_wo, t)
                        ht = h[:, bass.ds(t - 1, 1), :].squeeze(1)
                        nc.vector.tensor_tensor(ht, ht, bank[:, BX, 0:D], ALU.add).then_inc(s_res, 1)
                    if has(-1):
                        take(5, t + 1, o)

                steps(step, dve)

            @block.scalar
            def _(act):
                nc.scalar.preload_act_table(ACT.Exp)
                act.wait_ge(s_lsum, 1)
                nc.scalar.activation(lexp[:, :], lsum[:, :], ACT.Exp).then_inc(s_lexp, 1)

                def take(j, t, par):
                    act.wait_ge(s_fill, 6 * t + j + 1)
                    if j < 4:
                        dst = (qT, kT)[j // 2][:, par, 4 * (j % 2):4 * (j % 2) + 4, :]
                        nc.scalar.copy(dst, bank[:, BP, :].rearrange("p (c n) -> p c n", c=4)).then_inc(s_fa, 1)
                    else:
                        nc.scalar.copy(val[:, par, 512 * (j - 4):512 * (j - 3)], bank[:, BP, :]).then_inc(s_fa, 1)

                def softmax(n, q, first, last):
                    if first == 0:
                        act.wait_ge(s_max, n + 1)
                    for c in range(first, last):
                        at = (c % 4) * P
                        mm = nc.scalar.activation(prob[:, q, c, :], bank[:, 2 * q + c // 4, at:at + P], ACT.Exp,
                                                  bias=negmax[:, q, c:c + 1], accum_out=psum_[:, q, c:c + 1])
                    if last == 8:
                        mm.then_inc(s_exp, 1)

                def normed_high(n, q):
                    act.wait_ge(s_nT_ps, n + 1)
                    nc.scalar.copy(normedT_high[:, q], bank[:, BX, :].rearrange("p (c n) -> p c n", c=4)).then_inc(s_nT_high, 1)

                def squares(n, q):
                    act.wait_ge(s_pv, n + 1)
                    for c in range(4):
                        mm = nc.scalar.activation(junk[:, q, c, :], bank[:, BV, c * P:(c + 1) * P], ACT.Square,
                                                  accum_out=ssq[:, q, c:c + 1])
                    mm.then_inc(s_sq, 1)

                def step(t, p, has):
                    o = 1 - p
                    if has(-1):
                        take(0, t + 1, o)
                    if has(0):
                        softmax(2 * t, 0, 0, 8)
                    if has(-1):
                        take(1, t + 1, o)
                    if has(1):
                        normed_high(2 * t - 2, 0)
                        squares(2 * t - 1, 1)
                    if has(-1):
                        take(2, t + 1, o)
                    if has(0):
                        softmax(2 * t + 1, 1, 0, 2)
                    if has(1):
                        normed_high(2 * t - 1, 1)
                    if has(0):
                        softmax(2 * t + 1, 1, 2, 8)
                    if has(3):
                        act.wait_ge(g_neg, t - 2)
                        nc.scalar.activation(gexp[:, :], logit[:, :], ACT.Exp, bias=gnegmax[:, 0:1],
                                             accum_out=gsum[:, :]).then_inc(g_exp, 1)
                    if has(-2):
                        act.wait_ge(s_xnT, t + 3)
                        nc.scalar.copy(xnT_high[:, p], xnT[:, p]).then_inc(s_x_high, 1)
                    if has(-1):
                        take(4, t + 1, o)
                    if has(0):
                        squares(2 * t, 0)

                steps(step, act)


def expert_phase(nc, a, m, rows, out):
    bank, c128 = m["bank"], m["c128"]
    ident = c128[:, C_ID:C_ID + P]
    NC = CAP // P
    NH = HID // P
    with ExitStack() as ctx:
        def sb(name, shape, dt=F32):
            return ctx.enter_context(nc.sbuf_tensor(name, shape, dt))

        def sem(name):
            return ctx.enter_context(nc.semaphore(name))

        w1_raw = sb("w1_raw", [P, 2, HID])
        w2_raw = sb("w2_raw", [P, NH, D])
        w1_high, w1_low = sb("w1_high", [P, 2, HID], F32R), sb("w1_low", [P, 2, HID], F32R)
        w2_high, w2_low = sb("w2_high", [P, NH, D], F32R), sb("w2_low", [P, NH, D], F32R)
        b1 = sb("b1", [P, NE, NH])
        b1raw = sb("b1raw", [NE, HID])
        b2 = sb("b2", [P, 2, D])
        x = sb("x_rows", [P, 2, NC, ROW])
        gate = sb("gate", [P, 2, NC])
        token = sb("token", [P, 2, NC], U32)
        stats = sb("e_stats", [P, NC, 6])
        meanvar = sb("e_meanvar", [P, NC, 2])
        rstd = sb("e_rstd", [P, NC])
        xn = sb("e_xn", [P, NC, D])
        xT_high, xT_low = sb("e_xT_high", [P, 2, 2, CAP], F32R), sb("e_xT_low", [P, 2, 2, CAP], F32R)
        hidden = sb("e_hidden", [P, 4, CAP])
        hT_high, hT_low = sb("e_hT_high", [P, NH, CAP], F32R), sb("e_hT_low", [P, NH, CAP], F32R)
        yb = sb("e_yb", [P, 2, D])
        yg = sb("e_yg", [P, NC, D])
        y = sb("e_y", [P, NC, D])

        ld_w1, ld_w2 = sem("e_ld_w1"), sem("e_ld_w2")
        ld_b2, ld_x = ([sem(f"e_ld_{n}{i}") for i in range(2)] for n in ("b2_", "x_"))
        ld_b1, s_b1_ps, s_b1 = sem("e_ld_b1"), sem("e_b1_ps"), sem("e_b1")
        s_stat, s_tok, s_mean, s_var, s_rstd, s_xn, s_xT_ps, s_xT_high, s_xT_low = \
            sem("e_stat"), sem("e_tok"), sem("e_mean"), sem("e_var"), sem("e_rstd"), sem("e_norm"), sem("e_xT_ps"), \
            sem("e_xTh"), sem("e_xTl")
        s_w1_high, s_w1_low, s_w2_high, s_w2_low = sem("e_w1h"), sem("e_w1l"), sem("e_w2h"), sem("e_w2l")
        s_h_ps, s_h_high, s_h, s_h_act, s_h_low, s_h_low_v, s_y_ps, s_yb, s_yg, s_y = \
            sem("e_h_ps"), sem("e_hh"), sem("e_h"), sem("e_ha"), sem("e_hl"), sem("e_hlv"), sem("e_y_ps"), sem("e_ybs"), sem("e_ygs"), sem("e_ys")
        sent = [sem(f"e_sent{c}") for c in range(NC)]

        def quarter(w, i):
            return w[:, 2 * i:2 * i + 2, :].rearrange("p k n -> p (k n)")

        def steps(step, engine):
            def peeled(e):
                step(e, e % 2, lambda lag: 0 <= e - lag < NE)

            peeled(-1)
            peeled(0)
            with engine.Fori(0, NE // 2 - 1) as i:
                for p in (1, 0):
                    step(2 * i + (2 - p), p, lambda lag: True)
            peeled(NE - 1)

        BH = (0, 1, 6, 7)
        NP = 6
        NV = 5

        def wait_hidden(engine, e, n):
            if n < NV:
                engine.wait_ge(s_h, NV * e + n + 1)
            else:
                engine.wait_ge(s_h_act, (NH - NV) * e + n - NV + 1)

        with nc.Block() as block:
            @block.sync
            def _(sp):
                sp.dma_start(b1raw[:, :], a["L1_ffn_b1"]).then_inc(ld_b1, 16)
                def load_rows(e, q):
                    sp.dma_start(x[:, q], rows[bass.ds(CAP * (e + 1), CAP), :].rearrange("(c p) d -> p c d", p=P))\
                      .then_inc(ld_x[q], 16)

                def step(e, p, has):
                    q = 1 - p
                    if has(-1):
                        if has(1):
                            sp.wait_ge(s_y, NC * e)
                        if has(0):
                            load_rows(e, q)
                        sp.dma_start(b2[:, q, :], a["L1_ffn_b2"][bass.ds(e + 1, 1), :].to_broadcast([P, D]))\
                          .then_inc(ld_b2[q], 16)
                        if has(0):
                            sp.wait_ge(s_w1_low, e + 1)
                        sp.dma_start(w1_raw[:, :, :], a["L1_ffn_W1"][bass.ds(e + 1, 1)].squeeze(0)
                                     .rearrange("(k p) n -> p k n", p=P)).then_inc(ld_w1, 16)
                        if has(0):
                            sp.wait_ge(s_w2_low, 4 * e + 4)
                        sp.dma_start(w2_raw[:, :, :], a["L1_ffn_W2"][bass.ds(e + 1, 1)].squeeze(0)
                                     .rearrange("(k p) n -> p k n", p=P)).then_inc(ld_w2, 16)
                        if not has(0):
                            sp.wait_ge(m["scattered"][0], 16 * NT // 2)
                            sp.wait_ge(m["scattered"][1], 16 * NT // 2)
                            load_rows(e, q)

                steps(step, sp)
                for c in range(NC):
                    sp.wait_ge(sent[c], 16 * NE)

            @block.gpsimd
            def _(pool):
                last_token = pool.to_reg(NT * P - 1)
                pool.wait_ge(m["prefilled"], 16 * NT)

                def power(e):
                    pool.wait_ge(s_var, e + 2)
                    nc.gpsimd.tensor_tensor(rstd[:, :], rstd[:, :], m["halfneg"][:, 0:NC], ALU.pow).then_inc(s_rstd, 1)

                def send(c, p):
                    nc.gpsimd.indirect_dma_start(
                        out=out, out_offset=bass.IndirectOffsetOnAxis(ap=token[:, p, c:c + 1], axis=0),
                        in_=y[:, c, :], in_offset=None, bounds_check=last_token, oob_is_err=False).then_inc(sent[c], 16)

                def step(e, p, has):
                    if has(0):
                        for n in range(NP):
                            wait_hidden(pool, e, n)
                            nc.gpsimd.tensor_tensor(hT_low[:, n, :], hidden[:, n % 4, :], hT_high[:, n, :].bitcast(F32),
                                                    ALU.subtract).then_inc(s_h_low, 1)
                            if n == 2 and has(-1):
                                power(e)
                    else:
                        power(e)
                    if has(0):
                        for c in range(NC):
                            pool.wait_ge(s_yg, NC * e + c + 1)
                            if c == 1:
                                pool.wait_ge(s_tok, e + 1)
                            if has(1):
                                pool.wait_ge(sent[c], 16 * e)
                            if c or has(1):
                                pool.wait_ge(s_y, NC * e + c)
                            nc.gpsimd.tensor_tensor(y[:, c, :], yg[:, c, :], x[:, p, c, 0:D], ALU.add).then_inc(s_y, 1)
                            if c:
                                send(c - 1, p)
                            elif has(1):
                                send(NC - 1, 1 - p)

                steps(step, pool)
                pool.wait_ge(s_y, NC * NE)
                send(NC - 1, (NE - 1) % 2)

            @block.tensor
            def _(pe):
                pe.wait_ge(ld_b1, 16)
                for n in range(NH):
                    mm = nc.tensor.transpose(bank[:, 7, n * NE:(n + 1) * NE], b1raw[:, n * P:(n + 1) * P],
                                             c128[0:NE, C_ID:C_ID + NE])
                mm.then_inc(s_b1_ps, 1)

                def turn_rows(e, has):
                    pe.wait_ge(s_xn, e + 2)
                    for k in range(2):
                        if has(0):
                            pe.wait_ge(s_xT_low, 2 * e + 1 + k)
                        for c in range(NC):
                            mm = nc.tensor.transpose(bank[:, 4 + k, c * P:(c + 1) * P], xn[:, c, k * P:(k + 1) * P], ident)
                        mm.then_inc(s_xT_ps, 1)

                def step(e, p, has):
                    if not has(0):
                        turn_rows(e, has)
                    if has(0):
                        pe.wait_ge(s_xT_low, 2 * e + 2)
                        pe.wait_ge(s_w1_low, e + 1)
                        for n in range(NH):
                            if n >= 4:
                                wait_hidden(pe, e, n - 4)
                            elif has(1):
                                wait_hidden(pe, e - 1, n + 4)
                            at = slice(n * P, (n + 1) * P)
                            for k in range(2):
                                nc.tensor.matmul(bank[:, BH[n % 4], :], w1_low[:, k, at], xT_high[:, p, k, :],
                                                 start=(k == 0), stop=False)
                                nc.tensor.matmul(bank[:, BH[n % 4], :], w1_high[:, k, at], xT_low[:, p, k, :],
                                                 start=False, stop=False)
                                mm = nc.tensor.matmul(bank[:, BH[n % 4], :], w1_high[:, k, at], xT_high[:, p, k, :],
                                                      start=False, stop=(k == 1))
                            mm.then_inc(s_h_ps, 1)
                    if has(0):
                        pe.wait_ge(s_w2_low, 4 * e + 4)
                        pe.wait_ge(s_h_high, NH * e + NH - 1)
                        for c in range(NC):
                            if c >= 2 or has(1):
                                pe.wait_ge(s_yb, NC * e + c - 1)
                            at = slice(c * P, (c + 1) * P)
                            for n in range(NH):
                                if c == 0 and n == NH - 1:
                                    pe.wait_ge(s_h_high, NH * e + NH)
                                nc.tensor.matmul(bank[:, 2 + c % 2, 0:D], hT_high[:, n, at], w2_low[:, n, :],
                                                 start=(n == 0), stop=False)
                                nc.tensor.matmul(bank[:, 2 + c % 2, 0:D], hT_high[:, n, at], w2_high[:, n, :],
                                                 start=False, stop=False)
                            if c == 0 and has(-1):
                                turn_rows(e, has)
                            if c == 0:
                                pe.wait_ge(s_h_low, NP * e + NP)
                                pe.wait_ge(s_h_low_v, (NH - NP) * (e + 1))
                            for n in range(NH):
                                mm = nc.tensor.matmul(bank[:, 2 + c % 2, 0:D], hT_low[:, n, at], w2_high[:, n, :],
                                                      start=False, stop=(n == NH - 1))
                            mm.then_inc(s_y_ps, 1)

                steps(step, pe)

            @block.vector
            def _(dve):
                dve.wait_ge(s_b1_ps, 1)
                nc.vector.tensor_copy(b1[:, :, :], bank[:, 7, 0:NH * NE].rearrange("p (n e) -> p e n", e=NE)).then_inc(s_b1, 1)

                def statistics(e, q):
                    dve.wait_ge(ld_x[q], 8 * (e + 1 - q) + 16)
                    for c in range(NC):
                        mm = nc.vector.bn_stats(stats[:, c, :], x[:, q, c, 0:D])
                    mm.then_inc(s_stat, 1)
                    dve.wait_ge(s_stat, e + 2)
                    nc.vector.tensor_copy(gate[:, q, :], x[:, q, :, D + 1])
                    for c in range(NC):
                        mm = nc.vector.bn_aggr(meanvar[:, c, :], stats[:, c, :])
                    mm.then_inc(s_mean, 1)
                    dve.wait_ge(s_mean, e + 2)
                    nc.vector.tensor_scalar(rstd[:, :], meanvar[:, :, 1], EPS, None, ALU.add).then_inc(s_var, 1)

                def norm(e, q):
                    dve.wait_ge(s_rstd, e + 2)
                    for c in range(NC):
                        mm = nc.vector.tensor_scalar(xn[:, c, :], x[:, q, c, 0:D], meanvar[:, c, 0:1], rstd[:, c:c + 1],
                                                     ALU.subtract, ALU.mult)
                    mm.then_inc(s_xn, 1)

                def weigh(c, e, p, has):
                    dve.wait_ge(s_y_ps, NC * e + c + 1)
                    nc.vector.tensor_tensor(yb[:, c % 2, :], bank[:, 2 + c % 2, 0:D], b2[:, p, :], ALU.add)\
                      .then_inc(s_yb, 1)
                    if has(1):
                        dve.wait_ge(s_y, NC * (e - 1) + c + 1)
                    dve.wait_ge(s_yb, NC * e + c + 1)
                    nc.vector.tensor_scalar(yg[:, c, :], yb[:, c % 2, :], gate[:, p, c:c + 1], None, ALU.mult)\
                      .then_inc(s_yg, 1)

                def step(e, p, has):
                    q = 1 - p
                    if has(0):
                        for n in range(NH):
                            if n < NV:
                                if n >= 4:
                                    dve.wait_ge(s_h_low, NP * e + n - 3)
                                elif has(1) and n + 4 < NP:
                                    dve.wait_ge(s_h_low, NP * (e - 1) + n + 5)
                                elif has(1):
                                    dve.wait_ge(s_h_low_v, (NH - NP) * (e - 1) + n + 5 - NP)
                                dve.wait_ge(s_h_high, NH * e + n + 1)
                                nc.vector.tensor_scalar(hidden[:, n % 4, :], bank[:, BH[n % 4], :],
                                                        b1[:, bass.ds(e, 1), n:n + 1].squeeze(1), 0.0, ALU.add, ALU.max)\
                                  .then_inc(s_h, 1)
                            if n < 4:
                                dve.wait_ge(s_w2_high, 4 * e + n + 1)
                                nc.vector.tensor_tensor(quarter(w2_low, n), quarter(w2_raw, n),
                                                        quarter(w2_high, n).bitcast(F32), ALU.subtract).then_inc(s_w2_low, 1)
                            if n >= NP:
                                wait_hidden(dve, e, n)
                                nc.vector.tensor_tensor(hT_low[:, n, :], hidden[:, n % 4, :], hT_high[:, n, :].bitcast(F32),
                                                        ALU.subtract).then_inc(s_h_low_v, 1)
                            if n == 2 and has(-1):
                                statistics(e, q)
                            if n == 4 and has(-1):
                                norm(e, q)
                    else:
                        statistics(e, q)
                        norm(e, q)
                    if has(0):
                        dve.wait_ge(ld_b2[p], 8 * (e - p) + 16)
                        weigh(0, e, p, has)
                    if has(-1):
                        dve.wait_ge(s_w1_high, e + 2)
                        nc.vector.tensor_tensor(w1_low[:, :, :], w1_raw[:, :, :], w1_high[:, :, :].bitcast(F32),
                                                ALU.subtract).then_inc(s_w1_low, 1)
                        for k in range(2):
                            dve.wait_ge(s_xT_high, 2 * e + 3 + k)
                            nc.vector.tensor_tensor(xT_low[:, q, k, :], bank[:, 4 + k, :], xT_high[:, q, k, :].bitcast(F32),
                                                    ALU.subtract).then_inc(s_xT_low, 1)
                    if has(0):
                        for c in range(1, NC):
                            weigh(c, e, p, has)
                    if has(-1):
                        if has(1):
                            dve.wait_ge(sent[NC - 1], 16 * e)
                        nc.vector.tensor_copy(token[:, q, :], x[:, q, :, D]).then_inc(s_tok, 1)

                steps(step, dve)

            @block.scalar
            def _(act):
                nc.scalar.preload_act_table(ACT.Relu)
                act.wait_ge(s_b1, 1)

                def step(e, p, has):
                    q = 1 - p
                    if has(0):
                        for n in range(NH):
                            if n >= NV:
                                act.wait_ge(s_h_low, NP * e + n - 3)
                            act.wait_ge(s_h_ps, NH * e + n + 1)
                            nc.scalar.activation(hT_high[:, n, :], bank[:, BH[n % 4], :], ACT.Relu,
                                                 bias=b1[:, bass.ds(e, 1), n:n + 1].squeeze(1)).then_inc(s_h_high, 1)
                            if n >= NV:
                                nc.scalar.activation(hidden[:, n % 4, :], bank[:, BH[n % 4], :], ACT.Relu,
                                                     bias=b1[:, bass.ds(e, 1), n:n + 1].squeeze(1)).then_inc(s_h_act, 1)
                            if n < 4:
                                act.wait_ge(ld_w2, 16 * e + 16)
                                nc.scalar.copy(quarter(w2_high, n), quarter(w2_raw, n)).then_inc(s_w2_high, 1)
                    if has(-1):
                        act.wait_ge(ld_w1, 16 * e + 32)
                        nc.scalar.copy(w1_high[:, :, :], w1_raw[:, :, :]).then_inc(s_w1_high, 1)
                        for k in range(2):
                            act.wait_ge(s_xT_ps, 2 * e + 3 + k)
                            nc.scalar.copy(xT_high[:, q, k, :], bank[:, 4 + k, :]).then_inc(s_xT_high, 1)

                steps(step, act)


def shape_constants():
    import numpy as np

    c = np.zeros((P, C_COLS), np.float32)
    r = np.arange(P)
    c[:, C_ID:C_ID + P] = np.eye(P)
    c[:, C_MASK:C_MASK + P] = np.where(r[None, :] <= r[:, None], 0.0, MASKED)
    c[:, C_TRI:C_TRI + P] = r[:, None] < r[None, :]
    c[:, C_VOC:C_VOC + P] = r[None, :] % V
    c[:, C_EXP:C_EXP + NE] = np.arange(NE)[None, :]
    c[:, C_TOK:C_TOK + NT] = r[:, None] + P * np.arange(NT)[None, :]
    c[:, C_VID] = r % V
    c[:, C_HALF] = np.where(r >= V, -1.0, 0.0)
    c[:, C_LOW] = np.where(r % 32 >= 16, -1.0, 0.0)
    c2 = np.zeros((V, C2_COLS), np.float32)
    for t in range(NFRAME):
        for n in range(V):
            s = V * t + n - V // 2
            s = -s if s < 0 else (2 * (P - 1) - s if s >= P else s)
            c2[n, C2_FRAME + P * t + s] = 1.0
    n, f = np.arange(V)[:, None], np.arange(NFREQ)[None, :]
    c2[:, C2_DFT:C2_DFT + NFREQ] = np.cos(2 * np.pi * n * f / V)
    c2[:, C2_DFT + NFREQ:C2_DFT + NREIM] = np.sin(2 * np.pi * n * f / V)
    wi = np.zeros((NFRAME + 1, P), np.float32)
    at = np.clip((np.arange(P) + 0.5) * (NFRAME / P) - 0.5, 0.0, NFRAME - 1.0)
    lo = np.floor(at).astype(int)
    hi = np.minimum(lo + 1, NFRAME - 1)
    w = (at - lo).astype(np.float32)
    np.add.at(wi, (lo, np.arange(P)), 1.0 - w)
    np.add.at(wi, (hi, np.arange(P)), w)
    wi[NFRAME] = 1.0
    return {"c_128": c, "c_64": c2, "c_interp": wi}


_INS = ['x', 'L0_tok_emb_table', 'L0_tok_proj_w', 'L0_tok_proj_b', 'L0_tok_window', 'L0_attn_w_attn',
        'L0_attn_w_proj', 'L0_ffn_ternary_weight', 'L0_ffn_bias', 'L0_ffn_act_scale', 'L1_attn_Wq', 'L1_attn_Wk',
        'L1_attn_Wv', 'L1_attn_Wo', 'L1_attn_lq1', 'L1_attn_lk1', 'L1_attn_lq2', 'L1_attn_lk2', 'L1_attn_subln_w',
        'L1_ffn_Wg', 'L1_ffn_bg', 'L1_ffn_W1', 'L1_ffn_b1', 'L1_ffn_W2', 'L1_ffn_b2']


def kernel(**inputs):
    import numpy as _np
    import concourse.bacc as _bacc
    from concourse.bass_utils import run_bass_kernel_spmd as _run

    nc = _bacc.Bacc("TRN2", target_bir_lowering=False, num_devices=1)
    arrays, args = {}, {}
    held = {name: _np.ascontiguousarray(inputs[name]) for name in _INS}
    held["L0_ffn_act_scale"] = held["L0_ffn_act_scale"].reshape(1)
    held.update(shape_constants())
    for name, a in held.items():
        arrays[f"in_{name}"] = a
        args[name] = nc.dram_tensor(f"in_{name}", a.shape, mybir.dt.from_np(a.dtype), kind="ExternalInput").ap()
    out = nc.dram_tensor("out_0", (NT * P, D), F32, kind="ExternalOutput").ap()
    rows = nc.dram_tensor("dispatched_rows", (NE * CAP, ROW), F32, kind="Internal").ap()
    tower_kernel(nc, args, rows, out)
    r = _run(nc, [arrays], core_ids=[0])
    return r.results[0]["out_0"].reshape(NT, P, D)
```
